# Optimizing a Trainium2 kernel written in Bass

```python
import numpy as np
import jax
import jax.numpy as jnp

def _softmax(x, axis=-1):
    return jax.nn.softmax(x, axis=axis)

def _gelu(x):
    return jax.nn.gelu(x, approximate=True)

def _silu(x):
    return jax.nn.silu(x)

def _sigmoid(x):
    return jax.nn.sigmoid(x)

def _layernorm(x, axis=-1, eps=1e-05):
    m = jnp.mean(x, axis=axis, keepdims=True)
    v = jnp.var(x, axis=axis, keepdims=True)
    return (x - m) / jnp.sqrt(v + eps)

def _scatter_add(tgt, idx, src, axis=0):
    return tgt.at[idx].add(src)

def _segment_sum(src, seg, n):
    return jax.ops.segment_sum(src, seg, n)
kernel_name = 'mk_gnn_resnorm_d1_gnn_r8_1375a5'

def setup_inputs(seed: int=0):
    np.random.seed(seed)
    _w = jnp.asarray

    def _rec_inputs():
        import jax
        import jax.numpy as jnp
        _gk = jax.random.key(seed)
        x = -0.000202 + 1 * jax.random.normal(jax.random.fold_in(_gk, 1), (6250, 128), jnp.float32)
        _s = jax.random.randint(jax.random.fold_in(_gk, 2), (50000,), 0, 6250, jnp.int32)
        _d = jax.random.randint(jax.random.fold_in(_gk, 3), (50000,), 0, 6250, jnp.int32)
        _loop = jnp.arange(6250, dtype=jnp.int32)
        src = jnp.concatenate([_s, _d, _loop])
        dst = jnp.concatenate([_d, _s, _loop])
        _o = jnp.argsort(dst, stable=True)
        src = src[_o]
        dst = dst[_o]
        edge_type_40 = jax.random.randint(jax.random.fold_in(_gk, 13), (106250,), 0, 40, jnp.int32)
        return (x, src, dst, edge_type_40)
    x, src, dst, edge_type_40 = _rec_inputs()

    def _L0_gnn_setup():
        import jax, jax.numpy as jnp
        import numpy as np
        N, E, D, R = (6250, 200000, 128, 40)
        DIFFUSION_STEPS = 1
        key = jax.random.key(seed)
        ks = jax.random.split(key, 8)
        return {'h': jax.random.normal(ks[0], (N, D), dtype=jnp.float32), 'rFeatures': jax.random.normal(ks[1], (R, D), dtype=jnp.float32), 'relation_weights': jax.random.normal(ks[2], (R, D, D), dtype=jnp.float32) * (1.0 / np.sqrt(D)), 'loop_weight': jax.random.normal(ks[3], (D, D), dtype=jnp.float32) * (1.0 / np.sqrt(D)), 'norm': jax.random.uniform(ks[4], (N, 1), dtype=jnp.float32), 'edge_src': jax.random.randint(ks[5], (E,), 0, N, dtype=jnp.int32), 'edge_dst': jax.random.randint(ks[6], (E,), 0, N, dtype=jnp.int32), 'edge_type': jax.random.randint(ks[7], (E,), 0, R, dtype=jnp.int32)}
    _L0_gnn_all = _L0_gnn_setup()
    _L0_gnn_in = {k: v for k, v in _L0_gnn_all.items() if k in ('rFeatures', 'relation_weights', 'loop_weight')}
    del _L0_gnn_all
    return {'x': x, 'src': src, 'dst': dst, 'edge_type_40': edge_type_40, 'L0_gnn_rFeatures': _L0_gnn_in['rFeatures'], 'L0_gnn_relation_weights': _L0_gnn_in['relation_weights'], 'L0_gnn_loop_weight': _L0_gnn_in['loop_weight']}

def reference(x, src, dst, edge_type_40, L0_gnn_rFeatures, L0_gnn_relation_weights, L0_gnn_loop_weight):
    import jax
    import jax.numpy as jnp

    def _L0_gnn_ref(h, rFeatures, relation_weights, loop_weight, norm, edge_src, edge_dst, edge_type):
        import jax, jax.numpy as jnp
        import numpy as np
        N, E, D, R = (6250, 200000, 128, 40)
        DIFFUSION_STEPS = 1
        n, d = h.shape
        r = relation_weights.shape[0]
        seg = edge_dst.astype(jnp.int32) * r + edge_type.astype(jnp.int32)
        for _ in range(DIFFUSION_STEPS):
            S = jax.ops.segment_sum(h[edge_src], seg, num_segments=n * r).reshape(n, r, d)
            cnt = jax.ops.segment_sum(jnp.ones(edge_src.shape, h.dtype), seg, num_segments=n * r).reshape(n, r)
            agg = jnp.einsum('nrd,rdf->nf', S, relation_weights) + cnt @ rFeatures
            h = agg * norm
        h = jax.nn.relu(h + h @ loop_weight)
        return h
    deg = jnp.maximum(jax.ops.segment_sum(jnp.ones(dst.shape, jnp.float32), dst, num_segments=6250), 1.0)
    deg_isqrt = deg ** (-0.5)
    x = _layernorm(x + _L0_gnn_ref(x, L0_gnn_rFeatures, L0_gnn_relation_weights, L0_gnn_loop_weight, deg_isqrt[:, None], src, dst, edge_type_40), axis=-1)
    return x

_drawn_inputs = setup_inputs


def setup_inputs(seed=0):
    import zlib

    import numpy as np

    out = dict(_drawn_inputs(seed))
    spreads = {}
    factors = {}
    for name, (base, spread) in spreads.items():
        noise = np.random.default_rng([zlib.crc32(name.encode()), seed]).standard_normal(out[name].shape)
        drawn = base * np.exp(spread * noise) if base else spread * noise
        out[name] = jnp.asarray(drawn.astype(out[name].dtype))
    for name, factor in factors.items():
        out[name] = (out[name] * factor).astype(out[name].dtype)
    return out
```

```python
from contextlib import ExitStack

import concourse.bass as bass
from concourse import mybir

ALU = mybir.AluOpType
AX = mybir.AxisListType
F32 = mybir.dt.float32
BF16 = mybir.dt.bfloat16
FP16 = mybir.dt.float16
I32 = mybir.dt.int32

P = 128
N, E, D, R = 6250, 106250, 128, 40
EPS = 1e-05

BLOCK = P
BLOCKS = -(-N // BLOCK)
LAST_ROWS = N - (BLOCKS - 1) * BLOCK
TPB = 17
TILES = BLOCKS * TPB
FULL = E // P
REST = E - FULL * P
assert TILES * P >= E

WIN = 12
COLS = R + 1
SEGS = 4
SEG = BLOCK + WIN
AHEAD = 3
COLS_T = TILES + AHEAD
POS = 20
HALF = 9
HALVES = [range(0, HALF), range(HALF, TPB)]
SUMS_FROM = 2
SUMS_TO = 15
LN_STEPS = 10


G_NODES = 448
G_CHUNKS = BLOCKS * BLOCK // G_NODES
G_RELS = 4
G_GROUPS = R // G_RELS
G_SETUP = 2
G_STEPS = 3 + R + 3 * G_CHUNKS
assert G_CHUNKS * G_NODES == BLOCKS * BLOCK and G_GROUPS * G_RELS == R

ROWS = 50
XP = N // ROWS
CHUNK = 10
CHUNKS = ROWS // CHUNK
PARTS = 3


def bank_of(k):
    return 4 if k == TPB - 1 else k % 4


def tiles_back(k):
    return TPB if k == TPB - 1 else 4 if k >= 4 else 5


def build(nc, x, src_main, src_rest, dst_main, dst_rest, type_main, type_rest, r_features, relation_w, loop_w, out):
    with ExitStack() as ctx:
        def sb(name, shape, dt):
            return ctx.enter_context(nc.sbuf_tensor(name, shape, dt))

        def psum(name, shape, dt=F32):
            return ctx.enter_context(nc.psum_tensor(name, shape, dt))

        def sem(name):
            return ctx.enter_context(nc.semaphore(name))

        x_parts = nc.dram_tensor("x_parts", [N, PARTS * D], BF16, kind="Internal").ap()

        w = sb("w", [P, COLS, D], F32)
        loop = sb("loop", [P, D], F32)
        ident = sb("ident", [P, P], F32)
        ones = sb("ones", [P, P], F32)
        src = sb("src", [P, COLS_T], I32)
        dst = sb("dst", [P, COLS_T], I32)
        typ = sb("typ", [P, COLS_T], I32)
        dst_f = sb("dst_f", [P, COLS_T], F32)
        typ_f = sb("typ_f", [P, COLS_T], F32)
        rel_f = sb("rel_f", [P, COLS_T], F32)
        key_f = sb("key_f", [P, COLS_T], F32)
        seg_i = sb("seg_i", [1, COLS_T], I32)
        off_i = sb("off_i", [1, COLS_T], I32)
        pos = sb("pos", [1, BLOCKS, POS], I32)
        iota = sb("iota", [P, R * WIN], FP16)
        iota_i = sb("iota_i", [P, R * WIN], I32)

        ring = sb("ring", [P, COLS, SEGS * SEG], F32)
        flat = ring[:].rearrange("p r n -> p (r n)")
        x_all = flat[0:XP, 0:ROWS * D]
        x_rem = flat[0:XP, ROWS * D:2 * ROWS * D]
        parts_all = flat[0:XP, 2 * ROWS * D:2 * ROWS * D + ROWS * D * PARTS // 2].bitcast(BF16).rearrange(
            "p (n c d) -> p n c d", c=PARTS, d=D)

        zeros = sb("zeros", [P, COLS, WIN], F32)
        blk_i = sb("blk_i", [1, TILES], I32)
        gap = sb("gap", [1, TILES], F32)
        worst = sb("worst", [P, 8], F32)
        broken = sb("broken", [P, 8], F32)
        broken_sum = sb("broken_sum", [1, 1], F32)
        general = sb("general", [1, 4], I32)

        g_at = [0]

        def piece(cols):
            g_at[0] += cols
            return flat[:, g_at[0] - cols:g_at[0]]

        g_agg, g_cnt = piece(BLOCKS * BLOCK), piece(BLOCKS * BLOCK)
        g_rows, g_rows_t, g_msg, g_type = (piece(P) for _ in range(4))
        g_hot, g_mask, g_from = piece(G_NODES), piece(R), piece(G_CHUNKS)
        idx = [sb(f"idx{h}", [P, len(HALVES[h])], I32) for h in range(2)]
        rows = sb("rows", [P, TPB, PARTS, D], BF16)
        hot = sb("hot", [P, TPB, R * WIN], BF16)
        hot_node = sb("hot_node", [P, TPB, WIN], BF16)
        hot_type = sb("hot_type", [P, TPB, P], BF16)

        agg_sb = sb("agg_sb", [P, BLOCK], F32)
        cnt_sb = sb("cnt_sb", [P, BLOCK], F32)
        deg = sb("deg", [P, 1], F32)
        deg_root = sb("deg_root", [P, 1], F32)
        var_eps = sb("var_eps", [P, 1], F32)
        var_root = sb("var_root", [P, 1], F32)
        norm = sb("norm", [P, 1], F32)
        h_sb = sb("h_sb", [P, D], F32)
        x_blk = sb("x_blk", [P, D], F32)
        y_sb = sb("y_sb", [P, D], F32)
        y_sum = sb("y_sum", [P, 1], F32)
        mean = sb("mean", [P, 1], F32)
        y_mid = sb("y_mid", [P, D], F32)
        y_sq = sb("y_sq", [P, D], F32)
        rstd = sb("rstd", [P, 1], F32)
        out_sb = sb("out_sb", [P, D], F32)

        win_ps = [psum(f"win_ps{b}", [P, COLS, WIN]) for b in range(5)]
        agg_ps = psum("agg_ps", [P, BLOCK])
        fin_ps = psum("fin_ps", [P, D + 1])
        g_prod_ps = psum("g_prod_ps", [P, G_RELS, D])
        g_turn_ps, g_agg_ps, g_cnt_ps = (
            win_ps[b][:].rearrange("p r n -> p (r n)")[:, 0:n] for b, n in ((2, P), (3, G_NODES), (4, G_NODES)))
        broken_ps = fin_ps[0:1, 0:8]
        lo_ps = [win_ps[b][:].rearrange("p r n -> p (r n)") for b in range(2)]

        x_loaded = [sem(f"x_loaded{c}") for c in range(CHUNKS)]
        edges_loaded = sem("edges_loaded")
        w_loaded = sem("w_loaded")
        padded = sem("padded")
        iota_done = sem("iota_done")
        const_done = sem("const_done")
        split_act = sem("split_act")
        split_dve = sem("split_dve")
        parts_stored = sem("parts_stored")
        meta = sem("meta")
        lo_spread = sem("lo_spread")
        pos_ready = sem("pos_ready")
        ring_zero = sem("ring_zero")
        broken_done = sem("broken_done")
        broken_summed = sem("broken_summed")
        path_known = sem("path_known")
        g_idx = sem("g_idx")
        g_gathered = sem("g_gathered")
        g_turned = sem("g_turned")
        g_copied = sem("g_copied")
        g_products = sem("g_products")
        g_step = sem("g_step")
        g_parts = sem("g_parts")
        idx_loaded = [sem(f"idx_loaded{h}") for h in range(2)]
        gathered = [sem(f"gathered{k}") for k in range(TPB)]
        hot_ready = sem("hot_ready")
        tile_done = sem("tile_done")
        copied = sem("copied")
        added = sem("added")
        merged = sem("merged")
        cleared = sem("cleared")
        sums_done = sem("sums_done")
        agg_ready = sem("agg_ready")
        fin_done = sem("fin_done")
        ln = sem("ln")
        rooted = sem("rooted")
        x_blk_loaded = sem("x_blk_loaded")
        stored = sem("stored")

        def at_least(eng, s, v):
            if not isinstance(v, int) or v > 0:
                eng.wait_ge(s, v)

        def known(i, low):
            return not isinstance(i, int) or i >= low

        def seg_start(eng, block):
            if isinstance(block, int):
                return block % SEGS * SEG
            return eng.snap((block % SEGS) * SEG, min_val=0, max_val=(SEGS - 1) * SEG)

        def positions(eng, regs, i):
            eng.load(regs, pos[0:1, i, 0:TPB] if isinstance(i, int) else pos[:].rearrange("p b k -> p (b k)")[
                0:1, bass.ds(i * POS, TPB)])
            return [eng.snap(r, min_val=0, max_val=SEGS * SEG - WIN - 1) for r in regs]

        def path(eng, in_order, in_general):
            eng.wait_ge(path_known, 1)
            which = eng.alloc_register(f"path_{eng.engine.name}")
            eng.load(which, general[0:1, 0:1])
            with eng.If_eq(which, 0):
                in_order()
            with eng.Else():
                in_general()

        def g_tiles(tile):
            def loop_on(eng):
                tile(0)
                with eng.Fori(1, TILES) as t:
                    tile(t)
            return loop_on

        def column(t):
            return slice(t, t + 1) if isinstance(t, int) else bass.ds(t, 1)

        def g_finish(eng, step):
            step(3, False, False, True)
            with eng.Fori(4, BLOCKS + 1) as i:
                step(i, False, False, True)
            for i in range(BLOCKS + 1, BLOCKS + 3):
                step(i, False, False, True)

        block = ctx.enter_context(nc.Block())

        @block.sync
        def _(sp):
            for t, main in ((src, src_main), (dst, dst_main), (typ, type_main)):
                sp.dma_start(t[:, 0:FULL], main).then_inc(edges_loaded, 16)
            x_v = x.rearrange("(p n) d -> p n d", n=ROWS)
            for c in range(CHUNKS):
                n = slice(c * CHUNK, (c + 1) * CHUNK)
                sp.dma_start(x_all.rearrange("p (n d) -> p n d", d=D)[:, n], x_v[:, n]).then_inc(x_loaded[c], 16)
                if c == 0:
                    sp.wait_ge(padded, 1)
                    for t, rest in ((src, src_rest), (dst, dst_rest), (typ, type_rest)):
                        sp.dma_start(t[0:REST, FULL:FULL + 1], rest).then_inc(edges_loaded, 16)
            sp.dma_start(w[:, 0:R, :], relation_w.rearrange("r d f -> d r f")).then_inc(w_loaded, 16)
            sp.wait_ge(const_done, 1)
            sp.dma_start(w[0:R, R, :], r_features).then_inc(w_loaded, 16)
            sp.dma_start(loop[:], loop_w).then_inc(w_loaded, 16)
            sp.dma_start(x_blk[:], x[0:P, :]).then_inc(x_blk_loaded, 16)
            parts_v = x_parts.rearrange("(p n) c -> p n c", n=ROWS)
            for c in range(CHUNKS):
                n = slice(c * CHUNK, (c + 1) * CHUNK)
                sp.wait_ge(split_dve, 2 * (c + 1))
                sp.dma_start(parts_v[:, n], parts_all[:, n].rearrange("p n c d -> p n (c d)")).then_inc(
                    parts_stored, 16)
            sp.wait_ge(edges_loaded, 6 * 16)

            def load_indices(i):
                for h, ks in enumerate(HALVES):
                    if known(i, 1):
                        for k in ks:
                            sp.wait_ge(gathered[k], i * 16)
                    t = i * TPB + ks[0]
                    sp.dma_start(idx[h][:], src[:, t:t + len(ks)] if isinstance(i, int) else src[
                        :, bass.ds(t, len(ks))]).then_inc(idx_loaded[h], 16)

            def in_order():
                load_indices(0)
                with sp.Fori(1, BLOCKS) as i:
                    load_indices(i)

            def g_load(t):
                if not isinstance(t, int):
                    sp.wait_ge(g_step, t * G_STEPS + G_SETUP)
                sp.dma_start(idx[0][:, 0:1], src[:, column(t)]).then_inc(g_idx, 16)

            path(sp, in_order, lambda: g_tiles(g_load)(sp))

        @block.gpsimd
        def _(pool):
            nc.gpsimd.memset(src[:, FULL:], 0)
            nc.gpsimd.memset(typ[:, FULL:], 0)
            nc.gpsimd.memset(dst[:, FULL:], N).then_inc(padded, 1)
            nc.gpsimd.memset(w[:, R, :], 0.0)
            nc.gpsimd.memset(ones[:], 1.0)
            nc.gpsimd.memset(ident[:], 0.0).then_inc(const_done, 1)
            nc.gpsimd.iota(iota_i[:], pattern=[[1, R * WIN]], base=0, channel_multiplier=0)
            nc.gpsimd.iota(blk_i[:], pattern=[[1, BLOCKS], [0, TPB]], base=0, channel_multiplier=0).then_inc(iota_done, 1)
            pool.wait_ge(const_done, 1)
            nc.gpsimd.affine_select(out=ident[:], in_=ident[:], compare_op=ALU.not_equal, fill=1.0, base=0,
                                    pattern=[[-1, P]], channel_multiplier=1).then_inc(const_done, 1)

            used = [pool.alloc_register(f"used{n}") for n in range(2)]
            pool.wait_ge(parts_stored, CHUNKS * 16)

            def gathers(i):
                for h, ks in enumerate(HALVES):
                    pool.wait_ge(idx_loaded[h], (i + 1) * 16)
                    for k in ks:
                        if known(i, 1):
                            now, then = used[k % 2], used[(k + 1) % 2]
                            pool.wait_ge(tile_done, now)
                            pool.reg_add(then, now, 1)
                        pool.indirect_dma_start(
                            rows[:, k].rearrange("p c d -> p (c d)"), None, x_parts,
                            bass.IndirectOffsetOnAxis(ap=idx[h][:, k - ks[0]:k - ks[0] + 1], axis=0),
                        ).then_inc(gathered[k], 16)

            def in_order():
                gathers(0)
                pool.reg_mov(used[TPB % 2], 1)
                with pool.Fori(1, BLOCKS) as i:
                    pool.reg_mov(used[0], used[TPB % 2])
                    gathers(i)

            def g_gather():
                pool.indirect_dma_start(g_rows, None, x, bass.IndirectOffsetOnAxis(ap=idx[0][:, 0:1], axis=0)).then_inc(
                    g_gathered, 16)

            def in_general():
                pool.wait_ge(g_step, G_SETUP)
                pool.wait_ge(g_idx, 16)
                g_gather()
                pool.reg_mov(used[1], 32)
                with pool.Fori(1, TILES):
                    pool.reg_mov(used[0], used[1])
                    pool.wait_ge(g_idx, used[0])
                    pool.reg_add(used[1], used[0], 16)
                    g_gather()

            path(pool, in_order, in_general)

        @block.scalar
        def _(act):
            for c in range(CHUNKS):
                n = slice(c * CHUNK, (c + 1) * CHUNK)
                m = slice(c * CHUNK * D, (c + 1) * CHUNK * D)
                act.wait_ge(x_loaded[c], 16)
                nc.scalar.copy(parts_all[:, n, 0, :], x_all[:, m].rearrange("p (n d) -> p n d", d=D)).then_inc(
                    split_act, 1)
                act.wait_ge(split_dve, 2 * c + 1)
                nc.scalar.copy(parts_all[:, n, 1, :], x_rem[:, m].rearrange("p (n d) -> p n d", d=D)).then_inc(
                    split_act, 1)
            regs = [act.alloc_register(f"act_pos{k}") for k in range(TPB)]

            def step(i, tiles, sums, fin):
                if tiles:
                    if isinstance(i, int):
                        act.wait_ge(pos_ready, 1)
                    start = positions(act, regs, i)
                for k in range(TPB):
                    if tiles:
                        t = i * TPB + k
                        if k == 0:
                            if isinstance(i, int) and i == 0:
                                act.wait_ge(ring_zero, 1)
                            if known(i, 3):
                                act.wait_ge(cleared, i - 2)
                        act.wait_ge(tile_done, t + 1)
                        at_least(act, copied, t)
                        nc.scalar.copy(ring[:, :, bass.ds(start[k] + 1, WIN - 1)],
                                       win_ps[bank_of(k)][:, :, 1:WIN]).then_inc(copied, 1)
                    if sums and k == 8:
                        c = i - 2
                        if known(i, 3):
                            act.wait_ge(merged, i - 2)
                        at_least(act, fin_done, c)
                        if not tiles or not known(i, 3):
                            act.wait_ge(copied, min(i, BLOCKS) * TPB)
                            act.wait_ge(added, min(i, BLOCKS) * TPB)
                        s = seg_start(act, c)
                        nc.scalar.copy(cnt_sb[:], ring[:, R, bass.ds(s, BLOCK)] if not isinstance(s, int) else
                                       ring[:, R, s:s + BLOCK]).then_inc(agg_ready, 1)
                    if sums and k == TPB - 1:
                        act.wait_ge(sums_done, i - 1)
                        nc.scalar.copy(agg_sb[:], agg_ps[:]).then_inc(agg_ready, 1)
                    if fin:
                        c = i - 3
                        if k == 5:
                            act.wait_ge(ln, c * LN_STEPS + 1)
                            nc.scalar.sqrt(deg_root[:], deg[:]).then_inc(rooted, 1)
                        if k == 10 and known_less(i, BLOCKS + 2):
                            act.wait_ge(ln, c * LN_STEPS + 4)
                            nxt = x[(c + 1) * P:min((c + 2) * P, N), :] if isinstance(c, int) else x[
                                bass.ds((c + 1) * P, P), :]
                            act.dma_start(x_blk[0:nxt.shape[0], :], nxt).then_inc(x_blk_loaded, 16)
                        if k == 12:
                            act.wait_ge(ln, c * LN_STEPS + 8)
                            nc.scalar.sqrt(var_root[:], var_eps[:]).then_inc(rooted, 1)
                        if k == 16:
                            act.wait_ge(ln, (c + 1) * LN_STEPS)
                            to = out[c * P:min((c + 1) * P, N), :] if isinstance(c, int) else out[bass.ds(c * P, P), :]
                            act.dma_start(to, out_sb[0:to.shape[0], :]).then_inc(stored, 16)

            def known_less(i, high):
                return not isinstance(i, int) or i < high

            def g_turn(t):
                act.wait_ge(g_turned, t + 1)
                nc.scalar.copy(g_rows_t, g_turn_ps).then_inc(g_copied, 1)

            def g_finish_step(i, tiles, sums, fin):
                c = i - 3
                at = slice(c * BLOCK, (c + 1) * BLOCK) if isinstance(c, int) else bass.ds(c * BLOCK, BLOCK)
                act.wait_ge(g_step, G_SETUP + TILES * G_STEPS)
                at_least(act, fin_done, c)
                nc.scalar.copy(cnt_sb[:], g_cnt[:, at]).then_inc(agg_ready, 1)
                nc.scalar.copy(agg_sb[:], g_agg[:, at]).then_inc(agg_ready, 1)
                step(i, tiles, sums, fin)

            def in_general():
                g_tiles(g_turn)(act)
                g_finish(act, g_finish_step)

            path(act, lambda: run(act, step), in_general)
            act.wait_ge(stored, BLOCKS * 16)

        @block.vector
        def _(dve):
            done = [0]

            def chain(ins):
                done[0] += 1
                ins.then_inc(meta, 1)
                dve.wait_ge(meta, done[0])

            nc.vector.memset(zeros[:], 0.0)
            dve.wait_ge(iota_done, 1)
            nc.vector.tensor_copy(iota[:], iota_i[:])
            dve.wait_ge(edges_loaded, 6 * 16)
            nc.vector.tensor_copy(typ_f[:], typ[:])
            chain(nc.vector.tensor_copy(dst_f[:], dst[:]))
            dve.wait_ge(lo_spread, 1)
            half = COLS_T // 2
            for b in range(2):
                c = slice(b * half, (b + 1) * half)
                ins = nc.vector.tensor_tensor(rel_f[:, c], dst_f[:, c], lo_ps[b][:, 0:half], ALU.subtract)
            chain(ins)
            first = half - 1
            nc.vector.tensor_tensor(key_f[:, 0:first], dst_f[:, 0:first], lo_ps[0][:, 1:half], ALU.subtract)
            chain(nc.vector.tensor_tensor(key_f[:, first:TILES], dst_f[:, first:TILES],
                                          lo_ps[1][:, 0:TILES - first], ALU.subtract))
            chain(nc.vector.memset(worst[:], 0.0))
            nc.vector.tensor_reduce(worst[:, 0:1], rel_f[:, 0:TILES], AX.X, ALU.max)
            nc.vector.tensor_reduce(worst[:, 1:2], rel_f[:, 0:TILES], AX.X, ALU.min)
            nc.vector.tensor_reduce(worst[:, 2:3], key_f[:, 0:TILES], AX.X, ALU.max)
            chain(nc.vector.tensor_tensor(gap[:], dst_f[0:1, 1:TILES + 1], dst_f[0:1, 0:TILES], ALU.subtract))
            nc.vector.tensor_reduce(worst[0:1, 3:4], gap[:], AX.X, ALU.max)
            nc.vector.tensor_copy(worst[0:1, 4:5], dst_f[0:1, 0:1])
            chain(nc.vector.tensor_scalar(seg_i[:], dst[0:1, :], 7, None, ALU.arith_shift_right))
            chain(nc.vector.tensor_tensor(gap[:], seg_i[:, 0:TILES], blk_i[:], ALU.subtract))
            nc.vector.tensor_reduce(worst[0:1, 5:6], gap[:], AX.X, ALU.max)
            chain(nc.vector.tensor_reduce(worst[0:1, 6:7], gap[:], AX.X, ALU.min))
            for n, (op, limit) in enumerate(((ALU.is_gt, WIN - 1), (ALU.is_lt, 0), (ALU.is_gt, 0), (ALU.is_gt, WIN - 1),
                                             (ALU.is_gt, WIN - 1), (ALU.is_gt, 1), (ALU.is_lt, -1), (ALU.is_gt, 0))):
                ins = nc.vector.tensor_scalar(broken[:, n:n + 1], worst[:, n:n + 1], float(limit), None, op)
            ins.then_inc(broken_done, 1)
            dve.wait_ge(broken_summed, 1)
            chain(nc.vector.reduce_sum(broken_sum[:], broken_ps, AX.X))
            nc.vector.tensor_copy(general[0:1, 0:1], broken_sum[:]).then_inc(path_known, 1)
            chain(nc.vector.scalar_tensor_tensor(out=key_f[:], in0=typ_f[:], scalar=float(WIN), in1=rel_f[:],
                                                 op0=ALU.mult, op1=ALU.add))
            chain(nc.vector.tensor_scalar(seg_i[:], dst[0:1, :], 7, SEGS - 1, ALU.arith_shift_right, ALU.bitwise_and))
            chain(nc.vector.tensor_scalar(off_i[:], dst[0:1, :], BLOCK - 1, None, ALU.bitwise_and))
            nc.vector.scalar_tensor_tensor(
                out=pos[:, :, 0:TPB], in0=seg_i[:, 0:TILES].rearrange("p (b k) -> p b k", k=TPB), scalar=float(SEG),
                in1=off_i[:, 0:TILES].rearrange("p (b k) -> p b k", k=TPB), op0=ALU.mult, op1=ALU.add,
            ).then_inc(pos_ready, 1)
            for c in range(CHUNKS):
                n = slice(c * CHUNK, (c + 1) * CHUNK)
                xv, rv = (a[:, c * CHUNK * D:(c + 1) * CHUNK * D].rearrange("p (n d) -> p n d", d=D)
                          for a in (x_all, x_rem))
                dve.wait_ge(split_act, 2 * c + 1)
                nc.vector.tensor_tensor(rv, xv, parts_all[:, n, 0, :], ALU.subtract).then_inc(split_dve, 1)
                dve.wait_ge(split_act, 2 * c + 2)
                nc.vector.tensor_tensor(parts_all[:, n, 2, :], rv, parts_all[:, n, 1, :], ALU.subtract).then_inc(
                    split_dve, 1)

            regs = [dve.alloc_register(f"dve_pos{k}") for k in range(TPB)]

            def one_hots(t, slot):
                at = slice(t, t + 1) if isinstance(t, int) else bass.ds(t, 1)
                if not isinstance(t, int) or t >= TPB:
                    dve.wait_ge(tile_done, t - TPB + 1)
                nc.vector.tensor_scalar(hot[:, slot], iota[:], key_f[:, at], None, ALU.is_equal)
                nc.vector.tensor_scalar(hot_node[:, slot], iota[:, 0:WIN], rel_f[:, at], None, ALU.is_equal)
                nc.vector.tensor_scalar(hot_type[:, slot], iota[:, 0:P], typ_f[:, at], None, ALU.is_equal).then_inc(
                    hot_ready, 1)

            def finish(c, k):
                if k == 3:
                    dve.wait_ge(fin_done, c + 1)
                    nc.vector.tensor_scalar(deg[:], fin_ps[:, D:D + 1], 1.0, None, ALU.max).then_inc(ln, 1)
                if k == 6:
                    dve.wait_ge(rooted, 2 * c + 1)
                    nc.vector.reciprocal(norm[:], deg_root[:]).then_inc(ln, 1)
                if k == 7:
                    dve.wait_ge(ln, c * LN_STEPS + 2)
                    nc.vector.tensor_scalar(h_sb[:], fin_ps[:, 0:D], norm[:], 0.0, ALU.mult, ALU.max).then_inc(ln, 1)
                if k == 8:
                    dve.wait_ge(ln, c * LN_STEPS + 3)
                    dve.wait_ge(x_blk_loaded, (c + 1) * 16)
                    nc.vector.tensor_tensor(y_sb[:], h_sb[:], x_blk[:], ALU.add).then_inc(ln, 1)
                if k == 9:
                    dve.wait_ge(ln, c * LN_STEPS + 4)
                    nc.vector.reduce_sum(y_sum[:], y_sb[:], AX.X).then_inc(ln, 1)
                    dve.wait_ge(ln, c * LN_STEPS + 5)
                    nc.vector.tensor_scalar(mean[:], y_sum[:], 1.0 / D, None, ALU.mult).then_inc(ln, 1)
                if k == 10:
                    dve.wait_ge(ln, c * LN_STEPS + 6)
                    nc.vector.tensor_scalar(y_mid[:], y_sb[:], mean[:], None, ALU.subtract).then_inc(ln, 1)
                if k == 11:
                    dve.wait_ge(ln, c * LN_STEPS + 7)
                    nc.vector.tensor_tensor_reduce(out=y_sq[:], in0=y_mid[:], in1=y_mid[:], scale=1.0 / D, scalar=EPS,
                                                   op0=ALU.mult, op1=ALU.add, accum_out=var_eps[:]).then_inc(ln, 1)
                if k == 13:
                    dve.wait_ge(rooted, 2 * c + 2)
                    nc.vector.reciprocal(rstd[:], var_root[:]).then_inc(ln, 1)
                if k == 14:
                    dve.wait_ge(ln, c * LN_STEPS + 9)
                    at_least(dve, stored, c * 16)
                    nc.vector.tensor_scalar(out_sb[:], y_mid[:], rstd[:], None, ALU.mult).then_inc(ln, 1)

            def step(i, tiles, sums, fin):
                c = i - 3
                if sums and known(i, 3):
                    last = i * TPB if tiles else BLOCKS * TPB
                    dve.wait_ge(copied, last)
                    dve.wait_ge(added, last)
                    head, tail = seg_start(dve, i - 2), seg_start(dve, i - 3)
                    nc.vector.tensor_tensor(
                        ring[:, :, bass.ds(head, WIN)], ring[:, :, bass.ds(head, WIN)],
                        ring[:, :, bass.ds(tail + BLOCK, WIN)], ALU.add).then_inc(merged, 1)
                    if tiles:
                        dve.wait_ge(merged, i - 2)
                        dve.wait_ge(sums_done, i - 2)
                        dve.wait_ge(agg_ready, 2 * (i - 2))
                        nc.vector.tensor_copy(ring[:, :, bass.ds(tail, WIN)], zeros[:])
                        nc.vector.tensor_copy(ring[:, :, bass.ds(tail + BLOCK, WIN)], zeros[:]).then_inc(cleared, 1)
                if tiles:
                    start = positions(dve, regs, i)
                for k in range(TPB):
                    if tiles:
                        t = i * TPB + k
                        one_hots(t + AHEAD, (k + AHEAD) % TPB)
                        dve.wait_ge(copied, t + 1)
                        at_least(dve, added, t)
                        if k == 0 and known(i, 3):
                            dve.wait_ge(cleared, i - 2)
                        a = ring[:, :, bass.ds(start[k], 1)]
                        nc.vector.tensor_tensor(a, a, win_ps[bank_of(k)][:, :, 0:1], ALU.add).then_inc(added, 1)
                    if fin:
                        finish(c, k)

            def in_order():
                dve.wait_ge(parts_stored, CHUNKS * 16)
                for s in range(SEGS):
                    nc.vector.tensor_copy(ring[:, :, s * SEG:s * SEG + WIN], zeros[:])
                    ins = nc.vector.tensor_copy(ring[:, :, s * SEG + BLOCK:(s + 1) * SEG], zeros[:])
                ins.then_inc(ring_zero, 1)
                dve.wait_ge(ring_zero, 1)
                dve.wait_ge(pos_ready, 1)
                for t in range(AHEAD):
                    one_hots(t, t)
                run(dve, step)

            def g_tile(t):
                n = [t * G_STEPS + G_SETUP]

                def then(ins):
                    n[0] = n[0] + 1
                    ins.then_inc(g_step, 1)
                    dve.wait_ge(g_step, n[0])

                then(nc.vector.tensor_scalar(g_mask, iota[:, 0:R], typ_f[:, column(t)], None, ALU.is_equal))
                then(nc.vector.tensor_scalar(g_type, iota[:, 0:P], typ_f[:, column(t)], None, ALU.is_equal))
                then(nc.vector.tensor_scalar(g_from, iota[:, 0:G_CHUNKS], -float(G_NODES), dst_f[:, column(t)], ALU.mult,
                                             ALU.add))
                for r in range(R):
                    if r % G_RELS == 0:
                        dve.wait_ge(g_products, t * G_GROUPS + r // G_RELS + 1)
                    product = g_prod_ps[:, r % G_RELS, :]
                    if r == 0:
                        then(nc.vector.tensor_scalar(g_msg, product, g_mask[:, 0:1], None, ALU.mult))
                    else:
                        then(nc.vector.scalar_tensor_tensor(out=g_msg, in0=product, scalar=g_mask[:, r:r + 1], in1=g_msg,
                                                            op0=ALU.mult, op1=ALU.add))
                for q in range(G_CHUNKS):
                    then(nc.vector.tensor_scalar(g_hot, iota[:, 0:G_NODES], g_from[:, q:q + 1], None, ALU.is_equal))
                    dve.wait_ge(g_parts, t * G_CHUNKS + q + 1)
                    at = slice(q * G_NODES, (q + 1) * G_NODES)
                    then(nc.vector.tensor_tensor(g_agg[:, at], g_agg[:, at], g_agg_ps, ALU.add))
                    then(nc.vector.tensor_tensor(g_cnt[:, at], g_cnt[:, at], g_cnt_ps, ALU.add))

            def in_general():
                dve.wait_ge(parts_stored, CHUNKS * 16)
                nc.vector.memset(g_agg, 0.0).then_inc(g_step, 1)
                nc.vector.memset(g_cnt, 0.0).then_inc(g_step, 1)
                dve.wait_ge(g_step, G_SETUP)
                g_tiles(g_tile)(dve)
                g_finish(dve, step)

            path(dve, in_order, in_general)

        @block.tensor
        def _(pe):
            pe.wait_ge(meta, 1)
            pe.wait_ge(const_done, 2)
            half = COLS_T // 2
            for b in range(2):
                ins = nc.tensor.matmul(lo_ps[b][:, 0:half], ones[0:1, :], dst_f[0:1, b * half:(b + 1) * half],
                                       start=True, stop=True)
            ins.then_inc(lo_spread, 1)
            pe.wait_ge(broken_done, 1)
            nc.tensor.matmul(broken_ps, ones[:, 0:1], broken[:], start=True, stop=True).then_inc(broken_summed, 1)
            pe.wait_ge(w_loaded, 3 * 16)

            def tile(i, k):
                t = i * TPB + k
                pe.wait_ge(gathered[k], (i + 1) * 16)
                pe.wait_ge(hot_ready, t + 1)
                free = t - tiles_back(k) + 1
                at_least(pe, copied, free)
                at_least(pe, added, free)
                ps = win_ps[bank_of(k)][:].rearrange("p r n -> p (r n)")
                for part in range(PARTS):
                    nc.tensor.matmul(ps[:, 0:R * WIN], rows[:, k, part, :], hot[:, k], start=(part == 0),
                                     stop=(part == PARTS - 1))
                nc.tensor.matmul(ps[:, R * WIN:], hot_type[:, k], hot_node[:, k], start=False, stop=True,
                                 skip_group_check=True).then_inc(tile_done, 1)

            def relations(i, rs, seg):
                for r in rs:
                    ins = nc.tensor.matmul(agg_ps[:], w[:, r, :], ring[:, r, bass.ds(seg, BLOCK)], start=(r == 0),
                                           stop=(r == COLS - 1))
                if COLS - 1 in rs:
                    ins.then_inc(sums_done, 1)

            slots = SUMS_TO - SUMS_FROM

            def step(i, tiles, sums, fin):
                if sums:
                    seg = seg_start(pe, i - 2)
                for k in range(TPB):
                    if tiles:
                        tile(i, k)
                    if fin and k == 1:
                        c = i - 3
                        pe.wait_ge(agg_ready, 2 * (c + 1))
                        at_least(pe, ln, (c - 1) * LN_STEPS + 3)
                        nc.tensor.matmul(fin_ps[:, D:D + 1], cnt_sb[:], ones[:, 0:1], start=True, stop=True)
                        nc.tensor.matmul(fin_ps[:, 0:D], agg_sb[:], ident[:], start=True, stop=False)
                        nc.tensor.matmul(fin_ps[:, 0:D], agg_sb[:], loop[:], start=False, stop=True).then_inc(fin_done, 1)
                    if sums and SUMS_FROM <= k < SUMS_TO:
                        if k == SUMS_FROM:
                            if known(i, 3):
                                pe.wait_ge(merged, i - 2)
                            else:
                                pe.wait_ge(copied, i * TPB)
                                pe.wait_ge(added, i * TPB)
                            at_least(pe, agg_ready, 2 * (i - 2))
                        j = k - SUMS_FROM
                        relations(i, range(COLS * j // slots, COLS * (j + 1) // slots), seg)

            def g_tile(t):
                pe.wait_ge(g_gathered, (t + 1) * 16)
                nc.tensor.transpose(g_turn_ps, g_rows, ident[:]).then_inc(g_turned, 1)
                pe.wait_ge(g_copied, t + 1)
                for j in range(G_GROUPS):
                    at_least(pe, g_step, t * G_STEPS + G_SETUP + 3 + j * G_RELS)
                    nc.tensor.matmul(g_prod_ps[:].rearrange("p r f -> p (r f)"), g_rows_t,
                                     w[:, j * G_RELS:(j + 1) * G_RELS, :].rearrange("p r f -> p (r f)"),
                                     start=True, stop=True).then_inc(g_products, 1)
                for q in range(G_CHUNKS):
                    pe.wait_ge(g_step, t * G_STEPS + G_SETUP + 3 + R + 3 * q + 1)
                    nc.tensor.matmul(g_agg_ps, g_msg, g_hot, start=True, stop=True)
                    nc.tensor.matmul(g_cnt_ps, g_type, g_hot, start=True, stop=True).then_inc(g_parts, 1)

            def in_general():
                g_tiles(g_tile)(pe)
                g_finish(pe, step)

            path(pe, lambda: run(pe, step), in_general)


def run(eng, step):
    for i in range(4):
        step(i, True, i >= 2, i >= 3)
    with eng.Fori(4, BLOCKS) as i:
        step(i, True, True, True)
    for i in range(BLOCKS, BLOCKS + 3):
        step(i, False, i < BLOCKS + 2, True)


_OUT = (N, D)


def kernel(x, src, dst, edge_type_40, L0_gnn_rFeatures, L0_gnn_relation_weights, L0_gnn_loop_weight):
    import numpy as np
    import concourse.bacc as bacc
    from concourse.bass_utils import run_bass_kernel_spmd

    nc = bacc.Bacc("TRN2", target_bir_lowering=False, num_devices=1)
    arrays = {"x": np.ascontiguousarray(x)}
    for name, a in (("src", src), ("dst", dst), ("type", edge_type_40)):
        a = np.asarray(a)
        arrays[f"{name}_main"] = np.ascontiguousarray(a[:FULL * P].reshape(FULL, P).T)
        arrays[f"{name}_rest"] = np.ascontiguousarray(a[FULL * P:].reshape(REST, 1))
    arrays["r_features"] = np.ascontiguousarray(L0_gnn_rFeatures)
    arrays["relation_w"] = np.ascontiguousarray(L0_gnn_relation_weights)
    arrays["loop_w"] = np.ascontiguousarray(L0_gnn_loop_weight)
    args = [nc.dram_tensor(k, a.shape, mybir.dt.from_np(a.dtype), kind="ExternalInput").ap() for k, a in arrays.items()]
    out = nc.dram_tensor("out", _OUT, F32, kind="ExternalOutput").ap()
    build(nc, *args, out)
    r = run_bass_kernel_spmd(nc, [arrays], core_ids=[0])
    return r.results[0]["out"]
```

```python
from contextlib import ExitStack

import concourse.bass as bass
from concourse import mybir

ALU = mybir.AluOpType
AX = mybir.AxisListType
F32 = mybir.dt.float32
BF16 = mybir.dt.bfloat16
FP16 = mybir.dt.float16
I32 = mybir.dt.int32
F32R = mybir.dt.float32r

P = 128
N, E, D, R = 6250, 106250, 128, 40
EPS = 1e-05

BLOCK = P
BLOCKS = -(-N // BLOCK)
LAST_ROWS = N - (BLOCKS - 1) * BLOCK
TPB = 17
TILES = BLOCKS * TPB
FULL = E // P
REST = E - FULL * P
assert TILES * P >= E

WIN = 12
COLS = R + 1
SEGS = 5
SEG = BLOCK + WIN
AHEAD = 5
COLS_T = TILES + TPB
POS = 20
POS_LOAD = 4
ROUND_SHIFT = 10
ROUND_MULT = -(-(1 << ROUND_SHIFT) // SEGS)
assert all(b * ROUND_MULT >> ROUND_SHIFT == b // SEGS for b in range(BLOCKS + 1))
HOTS = 9
HALF = 9
HALVES = [range(0, HALF), range(HALF, TPB)]
REUSE = 4
assert AHEAD >= REUSE
SUMS_FROM = 4
SUMS_TO = 16
LN_STEPS = 10


G_NODES = 448
G_CHUNKS = BLOCKS * BLOCK // G_NODES
G_RELS = 4
G_GROUPS = R // G_RELS
G_SETUP = 2
G_STEPS = 3 + R + 3 * G_CHUNKS
assert G_CHUNKS * G_NODES == BLOCKS * BLOCK and G_GROUPS * G_RELS == R

ROWS = 50
XP = N // ROWS
CHUNK = 10
CHUNKS = ROWS // CHUNK
PARTS = 2


def bank_of(k):
    return 4 if k == TPB - 1 else k % 4


def hot_of(k):
    return HOTS - 1 if k == TPB - 1 else k % (HOTS - 1)


def build(nc, x, src_main, src_rest, dst_main, dst_rest, type_main, type_rest, r_features, relation_w, loop_w, out):
    with ExitStack() as ctx:
        def sb(name, shape, dt):
            return ctx.enter_context(nc.sbuf_tensor(name, shape, dt))

        def psum(name, shape, dt=F32):
            return ctx.enter_context(nc.psum_tensor(name, shape, dt))

        def sem(name):
            return ctx.enter_context(nc.semaphore(name))

        x_parts = nc.dram_tensor("x_parts", [N, PARTS * D], F32, kind="Internal").ap()

        w = sb("w", [P, COLS, D], F32)
        loop = sb("loop", [P, D], F32)
        ident = sb("ident", [P, P], F32)
        ones = sb("ones", [P, P], F32)
        src = sb("src", [P, COLS_T], I32)
        dst_f = sb("dst_f", [P, COLS_T], F32)
        typ_f = sb("typ_f", [P, COLS_T], F32)
        rel_f = sb("rel_f", [P, COLS_T], F32)
        key_f = sb("key_f", [P, COLS_T], F32)
        pos = sb("pos", [1, BLOCKS * POS], I32)
        iota = sb("iota", [P, R * WIN], FP16)

        ring = sb("ring", [P, COLS, SEGS * SEG], F32)
        flat = ring[:].rearrange("p r n -> p (r n)")

        def pieces():
            at = 0
            while True:
                cols = yield (flat[:, at - cols:at] if at else None)
                at += cols

        def in_ring():
            made = pieces()
            next(made)
            return made.send

        piece = in_ring()
        x_all = piece(ROWS * D)[0:XP]
        parts_all = piece(ROWS * PARTS * D)[0:XP].bitcast(F32R).rearrange("p (n c d) -> p n c d", c=PARTS, d=D)
        dst, typ = (piece(COLS_T).bitcast(I32) for _ in range(2))
        seg_i, off_i = (piece(COLS_T)[0:1].bitcast(I32) for _ in range(2))
        gap = piece(TILES)[0:1]
        blk_i = piece(TILES)[0:1].bitcast(I32)
        iota_i = piece(R * WIN).bitcast(I32)

        zeros = sb("zeros", [P, COLS, WIN], F32)
        worst = sb("worst", [P, 8], F32)
        broken = sb("broken", [P, 8], F32)
        broken_sum = sb("broken_sum", [1, 1], F32)
        general = sb("general", [1, 4], I32)

        piece = in_ring()
        g_agg, g_cnt = piece(BLOCKS * BLOCK), piece(BLOCKS * BLOCK)
        g_rows, g_rows_t, g_msg, g_type = (piece(P) for _ in range(4))
        g_hot, g_mask, g_from = piece(G_NODES), piece(R), piece(G_CHUNKS)

        idx = [sb(f"idx{h}", [P, len(HALVES[h])], I32) for h in range(2)]
        rows = sb("rows", [P, TPB, PARTS, D], F32R)
        hot = sb("hot", [P, HOTS, R * WIN], F32R)
        hot_node = sb("hot_node", [P, TPB, WIN], BF16)
        hot_type = sb("hot_type", [P, TPB, P], BF16)

        agg_sb = sb("agg_sb", [P, BLOCK], F32)
        cnt_sb = sb("cnt_sb", [P, BLOCK], F32)
        deg = sb("deg", [P, 1], F32)
        deg_root = sb("deg_root", [P, 1], F32)
        var_eps = sb("var_eps", [P, 1], F32)
        var_root = sb("var_root", [P, 1], F32)
        norm = sb("norm", [P, 1], F32)
        h_sb = sb("h_sb", [P, D], F32)
        x_blk = sb("x_blk", [P, D], F32)
        y_sb = sb("y_sb", [P, D], F32)
        y_sum = sb("y_sum", [P, 1], F32)
        mean = sb("mean", [P, 1], F32)
        y_mid = sb("y_mid", [P, D], F32)
        y_sq = sb("y_sq", [P, D], F32)
        rstd = sb("rstd", [P, 1], F32)
        out_sb = sb("out_sb", [P, D], F32)

        win_ps = [psum(f"win_ps{b}", [P, COLS, WIN]) for b in range(5)]
        agg_ps = psum("agg_ps", [P, BLOCK])
        fin_ps = psum("fin_ps", [P, D + 1])
        g_prod_ps = psum("g_prod_ps", [P, G_RELS, D])
        g_turn_ps, g_agg_ps, g_cnt_ps = (
            win_ps[b][:].rearrange("p r n -> p (r n)")[:, 0:n] for b, n in ((2, P), (3, G_NODES), (4, G_NODES)))
        broken_ps = fin_ps[0:1, 0:8]
        lo_ps = [win_ps[b][:].rearrange("p r n -> p (r n)") for b in range(2)]

        x_loaded = [sem(f"x_loaded{c}") for c in range(CHUNKS)]
        edges_loaded = sem("edges_loaded")
        w_loaded = sem("w_loaded")
        padded = sem("padded")
        iota_done = sem("iota_done")
        const_done = sem("const_done")
        split_act = sem("split_act")
        split_dve = sem("split_dve")
        parts_stored = sem("parts_stored")
        meta = sem("meta")
        lo_spread = sem("lo_spread")
        pos_ready = sem("pos_ready")
        ring_zero = sem("ring_zero")
        broken_done = sem("broken_done")
        broken_summed = sem("broken_summed")
        path_known = sem("path_known")
        g_idx = sem("g_idx")
        g_gathered = sem("g_gathered")
        g_turned = sem("g_turned")
        g_copied = sem("g_copied")
        g_products = sem("g_products")
        g_step = sem("g_step")
        g_parts = sem("g_parts")
        idx_loaded = [sem(f"idx_loaded{h}") for h in range(2)]
        gathered = [sem(f"gathered{k}") for k in range(TPB)]
        types_ready = sem("types_ready")
        hot_ready = sem("hot_ready")
        tile_done = sem("tile_done")
        copied = sem("copied")
        added = sem("added")
        merged = sem("merged")
        cleared = sem("cleared")
        sums_done = sem("sums_done")
        agg_ready = sem("agg_ready")
        fin_done = sem("fin_done")
        ln = sem("ln")
        rooted = sem("rooted")
        x_blk_loaded = sem("x_blk_loaded")
        stored = sem("stored")

        def at_least(eng, s, v):
            if not isinstance(v, int) or v > 0:
                eng.wait_ge(s, v)

        def known(i, low):
            return not isinstance(i, int) or i >= low

        def seg_start(eng, block):
            if isinstance(block, int):
                return block % SEGS * SEG
            return eng.snap((block % SEGS) * SEG, min_val=0, max_val=(SEGS - 1) * SEG)

        def window(eng, regs, i, k):
            if k % POS_LOAD == 0:
                n = min(POS_LOAD, TPB - k)
                at = i * POS + k
                eng.load(regs[k:k + n], pos[0:1, at:at + n] if isinstance(i, int) else pos[0:1, bass.ds(at, n)])
            return eng.snap(regs[k], min_val=0, max_val=SEGS * SEG - WIN)

        def path(eng, in_order, in_general):
            eng.wait_ge(path_known, 1)
            which = eng.alloc_register(f"path_{eng.engine.name}")
            eng.load(which, general[0:1, 0:1])
            with eng.If_eq(which, 0):
                in_order()
            with eng.Else():
                in_general()

        def g_tiles(tile):
            def loop_on(eng):
                tile(0)
                with eng.Fori(1, TILES) as t:
                    tile(t)
            return loop_on

        def column(t):
            return slice(t, t + 1) if isinstance(t, int) else bass.ds(t, 1)

        def nodes(c):
            return slice(c * BLOCK, (c + 1) * BLOCK) if isinstance(c, int) else bass.ds(c * BLOCK, BLOCK)

        def g_finish(eng, step):
            step(3, False, False, True)
            with eng.Fori(4, BLOCKS + 1) as i:
                step(i, False, False, True)
            for i in range(BLOCKS + 1, BLOCKS + 3):
                step(i, False, False, True)

        block = ctx.enter_context(nc.Block())

        @block.sync
        def _(sp):
            for t, main in ((src, src_main), (dst, dst_main), (typ, type_main)):
                sp.dma_start(t[:, 0:FULL], main).then_inc(edges_loaded, 16)
            x_v = x.rearrange("(p n) d -> p n d", n=ROWS)
            for c in range(CHUNKS):
                n = slice(c * CHUNK, (c + 1) * CHUNK)
                sp.dma_start(x_all.rearrange("p (n d) -> p n d", d=D)[:, n], x_v[:, n]).then_inc(x_loaded[c], 16)
                if c == 0:
                    sp.wait_ge(padded, 1)
                    for t, rest in ((src, src_rest), (dst, dst_rest), (typ, type_rest)):
                        sp.dma_start(t[0:REST, FULL:FULL + 1], rest).then_inc(edges_loaded, 16)
            parts_v = x_parts.rearrange("(p n) c -> p n c", n=ROWS)
            for c in range(CHUNKS):
                n = slice(c * CHUNK, (c + 1) * CHUNK)
                sp.wait_ge(split_dve, c + 1)
                sp.dma_start(parts_v[:, n], parts_all[:, n].rearrange("p n c d -> p n (c d)").bitcast(F32)).then_inc(
                    parts_stored, 16)
            sp.dma_start(w[:, 0:R, :], relation_w.rearrange("r d f -> d r f")).then_inc(w_loaded, 16)
            sp.wait_ge(const_done, 1)
            sp.dma_start(w[0:R, R, :], r_features).then_inc(w_loaded, 16)
            sp.dma_start(loop[:], loop_w).then_inc(w_loaded, 16)
            sp.dma_start(x_blk[:], x[0:P, :]).then_inc(x_blk_loaded, 16)
            sp.wait_ge(edges_loaded, 6 * 16)

            def load_indices(i):
                for h, ks in enumerate(HALVES):
                    if known(i, 1):
                        for k in ks:
                            sp.wait_ge(gathered[k], i * 16)
                    t = i * TPB + ks[0]
                    sp.dma_start(idx[h][:], src[:, t:t + len(ks)] if isinstance(i, int) else src[
                        :, bass.ds(t, len(ks))]).then_inc(idx_loaded[h], 16)

            def in_order():
                load_indices(0)
                with sp.Fori(1, BLOCKS) as i:
                    load_indices(i)

            def g_load(t):
                if not isinstance(t, int):
                    sp.wait_ge(g_step, t * G_STEPS + G_SETUP)
                sp.dma_start(idx[0][:, 0:1], src[:, column(t)]).then_inc(g_idx, 16)

            path(sp, in_order, lambda: g_tiles(g_load)(sp))

        @block.gpsimd
        def _(pool):
            nc.gpsimd.memset(src[:, FULL:], 0)
            nc.gpsimd.memset(typ[:, FULL:], 0)
            nc.gpsimd.memset(dst[:, FULL:], N).then_inc(padded, 1)
            nc.gpsimd.memset(w[:, R, :], 0.0)
            nc.gpsimd.memset(ones[:], 1.0)
            nc.gpsimd.memset(ident[:], 0.0).then_inc(const_done, 1)
            nc.gpsimd.iota(iota_i, pattern=[[1, R * WIN]], base=0, channel_multiplier=0)
            nc.gpsimd.iota(blk_i, pattern=[[1, BLOCKS], [0, TPB]], base=0, channel_multiplier=0).then_inc(iota_done, 1)
            pool.wait_ge(const_done, 1)
            nc.gpsimd.affine_select(out=ident[:], in_=ident[:], compare_op=ALU.not_equal, fill=1.0, base=0,
                                    pattern=[[-1, P]], channel_multiplier=1).then_inc(const_done, 1)

            free = [pool.alloc_register(f"free{h}") for h in range(2)]
            pool.wait_ge(parts_stored, CHUNKS * 16)

            def gathers(i):
                for h, ks in enumerate(HALVES):
                    pool.wait_ge(idx_loaded[h], (i + 1) * 16)
                    if known(i, 1):
                        pool.wait_ge(tile_done, free[h])
                        pool.reg_add(free[1 - h], free[h], len(HALVES[1 - h]))
                    for k in ks:
                        pool.indirect_dma_start(
                            rows[:, k].rearrange("p c d -> p (c d)").bitcast(F32), None, x_parts,
                            bass.IndirectOffsetOnAxis(ap=idx[h][:, k - ks[0]:k - ks[0] + 1], axis=0),
                        ).then_inc(gathered[k], 16)

            def in_order():
                gathers(0)
                pool.reg_mov(free[0], HALF)
                with pool.Fori(1, BLOCKS) as i:
                    gathers(i)

            def g_gather():
                pool.indirect_dma_start(g_rows, None, x, bass.IndirectOffsetOnAxis(ap=idx[0][:, 0:1], axis=0)).then_inc(
                    g_gathered, 16)

            def in_general():
                pool.wait_ge(g_step, G_SETUP)
                pool.wait_ge(g_idx, 16)
                g_gather()
                want, then = (pool.alloc_register(f"g_want{n}") for n in range(2))
                pool.reg_mov(then, 2 * 16)
                with pool.Fori(1, TILES):
                    pool.reg_mov(want, then)
                    pool.wait_ge(g_idx, want)
                    pool.reg_add(then, want, 16)
                    g_gather()

            path(pool, in_order, in_general)

        @block.scalar
        def _(act):
            for c in range(CHUNKS):
                n = slice(c * CHUNK, (c + 1) * CHUNK)
                m = slice(c * CHUNK * D, (c + 1) * CHUNK * D)
                act.wait_ge(x_loaded[c], 16)
                nc.scalar.copy(parts_all[:, n, 0, :], x_all[:, m].rearrange("p (n d) -> p n d", d=D)).then_inc(
                    split_act, 1)
            regs = [act.alloc_register(f"act_pos{k}") for k in range(TPB)]

            def step(i, tiles, sums, fin):
                if tiles and isinstance(i, int):
                    act.wait_ge(pos_ready, 1)
                for k in range(TPB):
                    if tiles:
                        t = i * TPB + k
                        if k == 0:
                            if isinstance(i, int) and i == 0:
                                act.wait_ge(ring_zero, 1)
                            if known(i, 4):
                                act.wait_ge(cleared, i - 3)
                        start = window(act, regs, i, k)
                        act.wait_ge(tile_done, t + 1)
                        at_least(act, copied, t)
                        nc.scalar.copy(ring[:, :, bass.ds(start + 1, WIN - 1)],
                                       win_ps[bank_of(k)][:, :, 1:WIN]).then_inc(copied, 1)
                    if sums and k == 8:
                        c = i - 2
                        if known(i, 3):
                            act.wait_ge(merged, i - 2)
                        at_least(act, fin_done, c)
                        if not tiles or not known(i, 3):
                            act.wait_ge(copied, min(i, BLOCKS) * TPB)
                            act.wait_ge(added, min(i, BLOCKS) * TPB)
                        s = seg_start(act, c)
                        nc.scalar.copy(cnt_sb[:], ring[:, R, bass.ds(s, BLOCK)] if not isinstance(s, int) else
                                       ring[:, R, s:s + BLOCK]).then_inc(agg_ready, 1)
                    if sums and k == TPB - 1:
                        act.wait_ge(sums_done, i - 1)
                        nc.scalar.copy(agg_sb[:], agg_ps[:]).then_inc(agg_ready, 1)
                    if fin:
                        c = i - 3
                        if k == 5:
                            act.wait_ge(ln, c * LN_STEPS + 1)
                            nc.scalar.sqrt(deg_root[:], deg[:]).then_inc(rooted, 1)
                        if k == 10 and known_less(i, BLOCKS + 2):
                            act.wait_ge(ln, c * LN_STEPS + 4)
                            nxt = x[(c + 1) * P:min((c + 2) * P, N), :] if isinstance(c, int) else x[
                                bass.ds((c + 1) * P, P), :]
                            act.dma_start(x_blk[0:nxt.shape[0], :], nxt).then_inc(x_blk_loaded, 16)
                        if k == 12:
                            act.wait_ge(ln, c * LN_STEPS + 8)
                            nc.scalar.sqrt(var_root[:], var_eps[:]).then_inc(rooted, 1)
                        if k == 16:
                            act.wait_ge(ln, (c + 1) * LN_STEPS)
                            to = out[c * P:min((c + 1) * P, N), :] if isinstance(c, int) else out[bass.ds(c * P, P), :]
                            act.dma_start(to, out_sb[0:to.shape[0], :]).then_inc(stored, 16)

            def known_less(i, high):
                return not isinstance(i, int) or i < high

            def g_turn(t):
                act.wait_ge(g_turned, t + 1)
                nc.scalar.copy(g_rows_t, g_turn_ps).then_inc(g_copied, 1)

            def g_finish_step(i, tiles, sums, fin):
                c = i - 3
                act.wait_ge(g_step, G_SETUP + TILES * G_STEPS)
                at_least(act, fin_done, c)
                nc.scalar.copy(cnt_sb[:], g_cnt[:, nodes(c)]).then_inc(agg_ready, 1)
                act.wait_ge(sums_done, c + 1)
                nc.scalar.copy(agg_sb[:], agg_ps[:]).then_inc(agg_ready, 1)
                step(i, tiles, sums, fin)

            def in_general():
                g_tiles(g_turn)(act)
                g_finish(act, g_finish_step)

            path(act, lambda: run(act, step), in_general)
            act.wait_ge(stored, BLOCKS * 16)

        @block.vector
        def _(dve):
            done = [0]

            def chain(ins):
                done[0] += 1
                ins.then_inc(meta, 1)
                dve.wait_ge(meta, done[0])

            nc.vector.memset(zeros[:], 0.0)
            dve.wait_ge(iota_done, 1)
            nc.vector.tensor_copy(iota[:], iota_i)
            dve.wait_ge(edges_loaded, 6 * 16)
            nc.vector.tensor_copy(typ_f[:], typ)
            chain(nc.vector.tensor_copy(dst_f[:], dst))
            dve.wait_ge(lo_spread, 1)
            half = COLS_T // 2
            for b in range(2):
                c = slice(b * half, (b + 1) * half)
                ins = nc.vector.tensor_tensor(rel_f[:, c], dst_f[:, c], lo_ps[b][:, 0:half], ALU.subtract)
            chain(ins)
            for c in range(CHUNKS):
                n = slice(c * CHUNK, (c + 1) * CHUNK)
                dve.wait_ge(split_act, c + 1)
                nc.vector.tensor_tensor(
                    parts_all[:, n, 1, :], x_all[:, c * CHUNK * D:(c + 1) * CHUNK * D].rearrange("p (n d) -> p n d", d=D),
                    parts_all[:, n, 0, :].bitcast(F32), ALU.subtract).then_inc(split_dve, 1)

            first = half - 1
            nc.vector.tensor_tensor(key_f[:, 0:first], dst_f[:, 0:first], lo_ps[0][:, 1:half], ALU.subtract)
            chain(nc.vector.tensor_tensor(key_f[:, first:TILES], dst_f[:, first:TILES],
                                          lo_ps[1][:, 0:TILES - first], ALU.subtract))
            chain(nc.vector.memset(worst[:], 0.0))
            nc.vector.tensor_reduce(worst[:, 0:1], rel_f[:, 0:TILES], AX.X, ALU.max)
            nc.vector.tensor_reduce(worst[:, 1:2], rel_f[:, 0:TILES], AX.X, ALU.min)
            nc.vector.tensor_reduce(worst[:, 2:3], key_f[:, 0:TILES], AX.X, ALU.max)
            chain(nc.vector.tensor_tensor(gap, dst_f[0:1, 1:TILES + 1], dst_f[0:1, 0:TILES], ALU.subtract))
            nc.vector.tensor_reduce(worst[0:1, 3:4], gap, AX.X, ALU.max)
            nc.vector.tensor_copy(worst[0:1, 4:5], dst_f[0:1, 0:1])
            chain(nc.vector.tensor_scalar(seg_i[:], dst[0:1, :], 7, None, ALU.arith_shift_right))
            chain(nc.vector.tensor_tensor(gap, seg_i[:, 0:TILES], blk_i, ALU.subtract))
            nc.vector.tensor_reduce(worst[0:1, 5:6], gap, AX.X, ALU.max)
            chain(nc.vector.tensor_reduce(worst[0:1, 6:7], gap, AX.X, ALU.min))
            for n, (op, limit) in enumerate(((ALU.is_gt, WIN - 1), (ALU.is_lt, 0), (ALU.is_gt, 0), (ALU.is_gt, WIN - 1),
                                             (ALU.is_gt, WIN - 1), (ALU.is_gt, 1), (ALU.is_lt, -1), (ALU.is_gt, 0))):
                ins = nc.vector.tensor_scalar(broken[:, n:n + 1], worst[:, n:n + 1], float(limit), None, op)
            ins.then_inc(broken_done, 1)
            dve.wait_ge(broken_summed, 1)
            chain(nc.vector.reduce_sum(broken_sum[:], broken_ps, AX.X))
            nc.vector.tensor_copy(general[0:1, 0:1], broken_sum[:]).then_inc(path_known, 1)
            chain(nc.vector.scalar_tensor_tensor(out=key_f[:], in0=typ_f[:], scalar=float(WIN), in1=rel_f[:],
                                                 op0=ALU.mult, op1=ALU.add))
            rounds = seg_i[:, 0:TILES]
            chain(nc.vector.tensor_scalar(off_i, dst[0:1, :], BLOCK - 1, None, ALU.bitwise_and))
            chain(nc.vector.scalar_tensor_tensor(out=blk_i, in0=seg_i[:, 0:TILES], scalar=float(SEG),
                                                 in1=off_i[:, 0:TILES], op0=ALU.mult, op1=ALU.add))
            chain(nc.vector.tensor_scalar(rounds, rounds, float(ROUND_MULT), None, ALU.mult))
            chain(nc.vector.tensor_scalar(rounds, rounds, ROUND_SHIFT, None, ALU.arith_shift_right))
            nc.vector.scalar_tensor_tensor(
                out=pos[:].rearrange("p (b k) -> p b k", k=POS)[:, :, 0:TPB], in0=rounds.rearrange("p (b k) -> p b k", k=TPB), scalar=-float(SEGS * SEG),
                in1=blk_i.rearrange("p (b k) -> p b k", k=TPB), op0=ALU.mult, op1=ALU.add,
            ).then_inc(pos_ready, 1)
            regs = [dve.alloc_register(f"dve_pos{k}") for k in range(TPB)]

            def one_hot(t, buffer):
                nc.vector.tensor_scalar(hot[:, buffer], iota[:], key_f[:, column(t)], None, ALU.is_equal).then_inc(
                    hot_ready, 1)

            def one_hot_types(i, h):
                ks, t = HALVES[h], i * TPB + HALVES[h][0]
                n = len(ks)
                ts = slice(t, t + n) if isinstance(t, int) else bass.ds(t, n)
                at = slice(ks[0], ks[0] + n)
                nc.vector.tensor_tensor(
                    hot_node[:, at], iota[:, 0:WIN].unsqueeze(1).to_broadcast([P, n, WIN]),
                    rel_f[:, ts].unsqueeze(2).to_broadcast([P, n, WIN]), ALU.is_equal)
                nc.vector.tensor_tensor(
                    hot_type[:, at, 0:R], iota[:, 0:R].unsqueeze(1).to_broadcast([P, n, R]),
                    typ_f[:, ts].unsqueeze(2).to_broadcast([P, n, R]), ALU.is_equal).then_inc(types_ready, 1)

            def finish(c, k):
                if k == 3:
                    dve.wait_ge(fin_done, c + 1)
                    nc.vector.tensor_scalar(deg[:], fin_ps[:, D:D + 1], 1.0, None, ALU.max).then_inc(ln, 1)
                if k == 6:
                    dve.wait_ge(rooted, 2 * c + 1)
                    nc.vector.reciprocal(norm[:], deg_root[:]).then_inc(ln, 1)
                if k == 7:
                    dve.wait_ge(ln, c * LN_STEPS + 2)
                    nc.vector.tensor_scalar(h_sb[:], fin_ps[:, 0:D], norm[:], 0.0, ALU.mult, ALU.max).then_inc(ln, 1)
                if k == 8:
                    dve.wait_ge(ln, c * LN_STEPS + 3)
                    dve.wait_ge(x_blk_loaded, (c + 1) * 16)
                    nc.vector.tensor_tensor(y_sb[:], h_sb[:], x_blk[:], ALU.add).then_inc(ln, 1)
                if k == 9:
                    dve.wait_ge(ln, c * LN_STEPS + 4)
                    nc.vector.reduce_sum(y_sum[:], y_sb[:], AX.X).then_inc(ln, 1)
                    dve.wait_ge(ln, c * LN_STEPS + 5)
                    nc.vector.tensor_scalar(mean[:], y_sum[:], 1.0 / D, None, ALU.mult).then_inc(ln, 1)
                if k == 10:
                    dve.wait_ge(ln, c * LN_STEPS + 6)
                    nc.vector.tensor_scalar(y_mid[:], y_sb[:], mean[:], None, ALU.subtract).then_inc(ln, 1)
                if k == 11:
                    dve.wait_ge(ln, c * LN_STEPS + 7)
                    nc.vector.tensor_tensor_reduce(out=y_sq[:], in0=y_mid[:], in1=y_mid[:], scale=1.0 / D, scalar=EPS,
                                                   op0=ALU.mult, op1=ALU.add, accum_out=var_eps[:]).then_inc(ln, 1)
                if k == 13:
                    dve.wait_ge(rooted, 2 * c + 2)
                    nc.vector.reciprocal(rstd[:], var_root[:]).then_inc(ln, 1)
                if k == 14:
                    dve.wait_ge(ln, c * LN_STEPS + 9)
                    at_least(dve, stored, c * 16)
                    nc.vector.tensor_scalar(out_sb[:], y_mid[:], rstd[:], None, ALU.mult).then_inc(ln, 1)

            def merge(i, tiles):
                dve.wait_ge(added, i * TPB if tiles else BLOCKS * TPB)
                if not tiles:
                    dve.wait_ge(copied, BLOCKS * TPB)
                head, tail = seg_start(dve, i - 2), seg_start(dve, i - 3)
                nc.vector.tensor_tensor(
                    ring[:, :, bass.ds(head, WIN)], ring[:, :, bass.ds(head, WIN)],
                    ring[:, :, bass.ds(tail + BLOCK, WIN)], ALU.add).then_inc(merged, 1)

            def clear(i):
                dve.wait_ge(merged, i - 2)
                dve.wait_ge(sums_done, i - 2)
                dve.wait_ge(agg_ready, 2 * (i - 2))
                old = seg_start(dve, i - 3)
                nc.vector.tensor_copy(ring[:, :, bass.ds(old, WIN)], zeros[:])
                nc.vector.tensor_copy(ring[:, :, bass.ds(old + BLOCK, WIN)], zeros[:]).then_inc(cleared, 1)

            def step(i, tiles, sums, fin):
                c = i - 3
                for k in range(TPB):
                    if sums and known(i, 3) and k == 1:
                        merge(i, tiles)
                    if tiles:
                        t = i * TPB + k
                        if k == 4:
                            one_hot_types(i, 1)
                        if k == 8 and known(i, 3):
                            clear(i)
                        if k == 13:
                            one_hot_types(i + 1, 0)
                        one_hot(t + AHEAD, hot_of((k + AHEAD) % TPB))
                        start = window(dve, regs, i, k)
                        dve.wait_ge(copied, t + 1)
                        at_least(dve, added, t)
                        if k == 0 and known(i, 4):
                            dve.wait_ge(cleared, i - 3)
                        a = ring[:, :, bass.ds(start, 1)]
                        nc.vector.tensor_tensor(a, a, win_ps[bank_of(k)][:, :, 0:1], ALU.add).then_inc(added, 1)
                    if fin:
                        finish(c, k)

            def in_order():
                dve.wait_ge(parts_stored, CHUNKS * 16)
                dve.wait_ge(pos_ready, 1)
                for s in range(SEGS):
                    nc.vector.tensor_copy(ring[:, :, s * SEG:s * SEG + WIN], zeros[:])
                    ins = nc.vector.tensor_copy(ring[:, :, s * SEG + BLOCK:(s + 1) * SEG], zeros[:])
                ins.then_inc(ring_zero, 1)
                dve.wait_ge(ring_zero, 1)
                nc.vector.memset(hot_type[:, :, R:], 0.0)
                one_hot_types(0, 0)
                for t in range(AHEAD):
                    one_hot(t, hot_of(t))
                run(dve, step)

            def g_tile(t):
                n = [t * G_STEPS + G_SETUP]

                def then(ins):
                    n[0] = n[0] + 1
                    ins.then_inc(g_step, 1)
                    dve.wait_ge(g_step, n[0])

                then(nc.vector.tensor_scalar(g_mask, iota[:, 0:R], typ_f[:, column(t)], None, ALU.is_equal))
                then(nc.vector.tensor_scalar(g_type, iota[:, 0:P], typ_f[:, column(t)], None, ALU.is_equal))
                then(nc.vector.tensor_scalar(g_from, iota[:, 0:G_CHUNKS], -float(G_NODES), dst_f[:, column(t)], ALU.mult,
                                             ALU.add))
                for r in range(R):
                    if r % G_RELS == 0:
                        dve.wait_ge(g_products, t * G_GROUPS + r // G_RELS + 1)
                    product = g_prod_ps[:, r % G_RELS, :]
                    if r == 0:
                        then(nc.vector.tensor_scalar(g_msg, product, g_mask[:, 0:1], None, ALU.mult))
                    else:
                        then(nc.vector.scalar_tensor_tensor(out=g_msg, in0=product, scalar=g_mask[:, r:r + 1], in1=g_msg,
                                                            op0=ALU.mult, op1=ALU.add))
                for q in range(G_CHUNKS):
                    then(nc.vector.tensor_scalar(g_hot, iota[:, 0:G_NODES], g_from[:, q:q + 1], None, ALU.is_equal))
                    dve.wait_ge(g_parts, t * G_CHUNKS + q + 1)
                    at = slice(q * G_NODES, (q + 1) * G_NODES)
                    then(nc.vector.tensor_tensor(g_agg[:, at], g_agg[:, at], g_agg_ps, ALU.add))
                    then(nc.vector.tensor_tensor(g_cnt[:, at], g_cnt[:, at], g_cnt_ps, ALU.add))

            def in_general():
                dve.wait_ge(parts_stored, CHUNKS * 16)
                dve.wait_ge(pos_ready, 1)
                nc.vector.memset(g_agg, 0.0).then_inc(g_step, 1)
                nc.vector.memset(g_cnt, 0.0).then_inc(g_step, 1)
                dve.wait_ge(g_step, G_SETUP)
                g_tiles(g_tile)(dve)
                g_finish(dve, step)

            path(dve, in_order, in_general)

        @block.tensor
        def _(pe):
            pe.wait_ge(meta, 1)
            pe.wait_ge(const_done, 2)
            half = COLS_T // 2
            for b in range(2):
                ins = nc.tensor.matmul(lo_ps[b][:, 0:half], ones[0:1, :], dst_f[0:1, b * half:(b + 1) * half],
                                       start=True, stop=True)
            ins.then_inc(lo_spread, 1)
            pe.wait_ge(broken_done, 1)
            nc.tensor.matmul(broken_ps, ones[:, 0:1], broken[:], start=True, stop=True).then_inc(broken_summed, 1)
            pe.wait_ge(w_loaded, 3 * 16)

            def tile(i, k):
                t = i * TPB + k
                pe.wait_ge(gathered[k], (i + 1) * 16)
                if k in (0, HALF):
                    pe.wait_ge(types_ready, 2 * i + 1 + k // HALF)
                if known(t, REUSE):
                    pe.wait_ge(added, t - REUSE + 1)
                else:
                    pe.wait_ge(hot_ready, t + 1)
                ps = win_ps[bank_of(k)][:].rearrange("p r n -> p (r n)")
                for part in range(PARTS):
                    nc.tensor.matmul(ps[:, 0:R * WIN], rows[:, k, part, :], hot[:, hot_of(k)], start=(part == 0),
                                     stop=(part == PARTS - 1))
                nc.tensor.matmul(ps[:, R * WIN:], hot_type[:, k], hot_node[:, k], start=False, stop=True,
                                 skip_group_check=True).then_inc(tile_done, 1)

            def relations(i, rs, seg):
                for r in rs:
                    ins = nc.tensor.matmul(agg_ps[:], w[:, r, :], ring[:, r, bass.ds(seg, BLOCK)], start=(r == 0),
                                           stop=(r == COLS - 1))
                if COLS - 1 in rs:
                    ins.then_inc(sums_done, 1)

            slots = SUMS_TO - SUMS_FROM

            def step(i, tiles, sums, fin):
                if sums:
                    seg = seg_start(pe, i - 2)
                for k in range(TPB):
                    if tiles:
                        tile(i, k)
                    if fin and k == 2:
                        c = i - 3
                        pe.wait_ge(agg_ready, 2 * (c + 1))
                        at_least(pe, ln, (c - 1) * LN_STEPS + 3)
                        nc.tensor.matmul(fin_ps[:, D:D + 1], cnt_sb[:], ones[:, 0:1], start=True, stop=True)
                        nc.tensor.matmul(fin_ps[:, 0:D], agg_sb[:], ident[:], start=True, stop=False)
                        nc.tensor.matmul(fin_ps[:, 0:D], agg_sb[:], loop[:], start=False, stop=True).then_inc(fin_done, 1)
                    if sums and SUMS_FROM <= k < SUMS_TO:
                        if k == SUMS_FROM:
                            if known(i, 3):
                                pe.wait_ge(merged, i - 2)
                            else:
                                pe.wait_ge(added, i * TPB)
                            at_least(pe, agg_ready, 2 * (i - 2))
                        j = k - SUMS_FROM
                        relations(i, range(COLS * j // slots, COLS * (j + 1) // slots), seg)

            def g_tile(t):
                pe.wait_ge(g_gathered, (t + 1) * 16)
                nc.tensor.transpose(g_turn_ps, g_rows, ident[:]).then_inc(g_turned, 1)
                pe.wait_ge(g_copied, t + 1)
                for j in range(G_GROUPS):
                    at_least(pe, g_step, t * G_STEPS + G_SETUP + 3 + j * G_RELS)
                    nc.tensor.matmul(g_prod_ps[:].rearrange("p r f -> p (r f)"), g_rows_t,
                                     w[:, j * G_RELS:(j + 1) * G_RELS, :].rearrange("p r f -> p (r f)"),
                                     start=True, stop=True).then_inc(g_products, 1)
                for q in range(G_CHUNKS):
                    pe.wait_ge(g_step, t * G_STEPS + G_SETUP + 3 + R + 3 * q + 1)
                    nc.tensor.matmul(g_agg_ps, g_msg, g_hot, start=True, stop=True)
                    nc.tensor.matmul(g_cnt_ps, g_type, g_hot, start=True, stop=True).then_inc(g_parts, 1)

            def g_finish_step(i, tiles, sums, fin):
                c = i - 3
                pe.wait_ge(g_step, G_SETUP + TILES * G_STEPS)
                at_least(pe, agg_ready, 2 * c)
                nc.tensor.matmul(agg_ps[:], w[:, R, :], g_cnt[:, nodes(c)], start=True, stop=False)
                nc.tensor.matmul(agg_ps[:], ident[:], g_agg[:, nodes(c)], start=False, stop=True).then_inc(sums_done, 1)
                step(i, tiles, sums, fin)

            def in_general():
                g_tiles(g_tile)(pe)
                g_finish(pe, g_finish_step)

            path(pe, lambda: run(pe, step), in_general)


def run(eng, step):
    for i in range(4):
        step(i, True, i >= 2, i >= 3)
    with eng.Fori(4, BLOCKS) as i:
        step(i, True, True, True)
    for i in range(BLOCKS, BLOCKS + 3):
        step(i, False, i < BLOCKS + 2, True)


_OUT = (N, D)


def kernel(x, src, dst, edge_type_40, L0_gnn_rFeatures, L0_gnn_relation_weights, L0_gnn_loop_weight):
    import numpy as np
    import concourse.bacc as bacc
    from concourse.bass_utils import run_bass_kernel_spmd

    nc = bacc.Bacc("TRN2", target_bir_lowering=False, num_devices=1)
    arrays = {"x": np.ascontiguousarray(x)}
    for name, a in (("src", src), ("dst", dst), ("type", edge_type_40)):
        a = np.asarray(a)
        arrays[f"{name}_main"] = np.ascontiguousarray(a[:FULL * P].reshape(FULL, P).T)
        arrays[f"{name}_rest"] = np.ascontiguousarray(a[FULL * P:].reshape(REST, 1))
    arrays["r_features"] = np.ascontiguousarray(L0_gnn_rFeatures)
    arrays["relation_w"] = np.ascontiguousarray(L0_gnn_relation_weights)
    arrays["loop_w"] = np.ascontiguousarray(L0_gnn_loop_weight)
    args = [nc.dram_tensor(k, a.shape, mybir.dt.from_np(a.dtype), kind="ExternalInput").ap() for k, a in arrays.items()]
    out = nc.dram_tensor("out", _OUT, F32, kind="ExternalOutput").ap()
    build(nc, *args, out)
    r = run_bass_kernel_spmd(nc, [arrays], core_ids=[0])
    return r.results[0]["out"]
```

```python
from contextlib import ExitStack

import concourse.bass as bass
from concourse import mybir

ALU = mybir.AluOpType
AX = mybir.AxisListType
F32 = mybir.dt.float32
BF16 = mybir.dt.bfloat16
FP16 = mybir.dt.float16
I32 = mybir.dt.int32
F32R = mybir.dt.float32r

P = 128
N, E, D, R = 6250, 106250, 128, 40
EPS = 1e-05

BANK = 512
BLOCK = P
BLOCKS = -(-N // BLOCK)
TPB = 17
TILES = BLOCKS * TPB
FULL = E // P
REST = E - FULL * P
assert TILES * P >= E

WIN = 12
COLS = R + 1
SEGS = 4
SEG = BLOCK + WIN
AHEAD = 5
COLS_T = TILES + TPB
POS = 20
POS_LOAD = 4
ROUND_SHIFT = 10
ROUND_MULT = -(-(1 << ROUND_SHIFT) // SEGS)
assert all(b * ROUND_MULT >> ROUND_SHIFT == b // SEGS for b in range(BLOCKS + 1))
HOTS = 9
HALF = 8
HALVES = [range(0, HALF), range(HALF, TPB)]
BANKS = 6
REUSE = 5
assert AHEAD >= REUSE
PAIR = 2
assert HALF % PAIR == 0
SAFE = 10
SUMS_FROM = 13
SUMS_LATE = 12
LN_STEPS = 10
W_LOAD = 5
W_LOADS = R // W_LOAD + 1
EARLY = 2
CHECKS = 7
CLEARS = range(0, 1), range(1, 2)


G_NODES = 448
G_CHUNKS = BLOCKS * BLOCK // G_NODES
G_RELS = 4
G_GROUPS = R // G_RELS
G_SETUP = 2
G_STEPS = 3 + R + 3 * G_CHUNKS
assert G_CHUNKS * G_NODES == BLOCKS * BLOCK and G_GROUPS * G_RELS == R

ROWS = 50
XP = N // ROWS
CHUNK = 10
CHUNKS = ROWS // CHUNK
PARTS = 2


def bank_of(k):
    return k % BANKS


assert all(bank_of(k) != bank_of(n % TPB) for k in range(TPB) for n in range(k + 1, k + REUSE))


def hot_of(k):
    return HOTS - 1 if k == TPB - 1 else k % (HOTS - 1)


def build(nc, x, src_main, src_rest, dst_main, dst_rest, type_main, type_rest, r_features, relation_w, loop_w, out):
    with ExitStack() as ctx:
        def sb(name, shape, dt):
            return ctx.enter_context(nc.sbuf_tensor(name, shape, dt))

        def psum(name, shape, dt=F32):
            return ctx.enter_context(nc.psum_tensor(name, shape, dt))

        def sem(name):
            return ctx.enter_context(nc.semaphore(name))

        x_parts = nc.dram_tensor("x_parts", [N, PARTS * D], F32, kind="Internal").ap()

        w = sb("w", [P, COLS, D], F32)
        loop = sb("loop", [P, D], F32)
        ident = sb("ident", [P, P], F32)
        ones = sb("ones", [P, P], F32)
        src = sb("src", [P, COLS_T], I32)
        dst_f = sb("dst_f", [P, COLS_T], F32)
        typ_f = sb("typ_f", [P, COLS_T], F32)
        rel_f = sb("rel_f", [P, COLS_T], F32)
        key_f = sb("key_f", [P, COLS_T], F32)
        pos = sb("pos", [1, BLOCKS * POS], I32)
        iota = sb("iota", [P, R * WIN], FP16)

        ring = sb("ring", [P, COLS, SEGS * SEG], F32)
        flat = ring[:].rearrange("p r n -> p (r n)")

        def pieces():
            at = 0
            while True:
                cols = yield (flat[:, at - cols:at] if at else None)
                at += cols

        def in_ring():
            made = pieces()
            next(made)
            return made.send

        piece = in_ring()
        x_all = piece(ROWS * D)[0:XP]
        parts_all = piece(ROWS * PARTS * D)[0:XP].bitcast(F32R).rearrange("p (n c d) -> p n c d", c=PARTS, d=D)
        dst, typ = (piece(COLS_T).bitcast(I32) for _ in range(2))
        head, head_next, head_seg, head_off, head_gap, blk_i, rounds, pos_2d = (
            piece(POS)[0:BLOCKS].bitcast(I32) for _ in range(8))
        after = piece(TILES)
        iota_i = piece(R * WIN).bitcast(I32)

        zeros = sb("zeros", [P, COLS, WIN], F32)
        worst = sb("worst", [P, CHECKS], F32)
        broken = sb("broken", [P, CHECKS], F32)
        broken_sum = sb("broken_sum", [1, 1], F32)
        general = sb("general", [1, 4], I32)

        piece = in_ring()
        g_agg, g_cnt = piece(BLOCKS * BLOCK), piece(BLOCKS * BLOCK)
        g_rows, g_rows_t, g_msg, g_type = (piece(P) for _ in range(4))
        g_hot, g_mask, g_from = piece(G_NODES), piece(R), piece(G_CHUNKS)

        idx = [sb(f"idx{h}", [P, len(HALVES[h])], I32) for h in range(2)]
        rows = sb("rows", [P, TPB, PARTS, D], F32R)
        first_rows = sb("first_rows", [P, TPB, PARTS, D], F32R)
        whole = w[:, 0:TPB, :]
        hot = sb("hot", [P, HOTS, R * WIN], F32R)
        hot_node = sb("hot_node", [P, TPB, WIN], BF16)
        hot_type = sb("hot_type", [P, TPB, P], BF16)

        agg_sb = sb("agg_sb", [P, BLOCK], F32)
        cnt_sb = sb("cnt_sb", [P, BLOCK], F32)
        deg = sb("deg", [P, 1], F32)
        deg_root = sb("deg_root", [P, 1], F32)
        var_eps = sb("var_eps", [P, 1], F32)
        var_root = sb("var_root", [P, 1], F32)
        norm = sb("norm", [P, 1], F32)
        h_sb = sb("h_sb", [P, D], F32)
        x_blk = sb("x_blk", [P, D], F32)
        y_sb = sb("y_sb", [P, D], F32)
        y_sum = sb("y_sum", [P, 1], F32)
        mean = sb("mean", [P, 1], F32)
        y_mid = sb("y_mid", [P, D], F32)
        y_sq = sb("y_sq", [P, D], F32)
        rstd = sb("rstd", [P, 1], F32)
        out_sb = sb("out_sb", [P, D], F32)

        banks = [psum(f"win_ps{b}", [P, BANK]) for b in range(BANKS)]
        win_ps = [b[:, 0:COLS * WIN].rearrange("p (r n) -> p r n", n=WIN) for b in banks]
        agg_ps = psum("agg_ps", [P, BLOCK])
        fin_ps = psum("fin_ps", [P, D + 1])
        g_prod_ps = banks[5]
        g_turn_ps, g_agg_ps, g_cnt_ps = (
            banks[b][:, 0:n] for b, n in ((2, P), (3, G_NODES), (4, G_NODES)))
        broken_ps = fin_ps[0:1, 0:CHECKS]
        lo_ps = banks[0:2]

        x_loaded = [sem(f"x_loaded{c}") for c in range(CHUNKS)]
        edges_loaded = sem("edges_loaded")
        src_loaded = sem("src_loaded")
        heads_loaded = sem("heads_loaded")
        w_loaded = sem("w_loaded")
        loop_loaded = sem("loop_loaded")
        loop_done = sem("loop_done")
        padded = sem("padded")
        iota_done = sem("iota_done")
        const_done = sem("const_done")
        split_act = sem("split_act")
        split_dve = sem("split_dve")
        first_high = sem("first_high")
        first_split = sem("first_split")
        parts_stored = sem("parts_stored")
        meta = sem("meta")
        lo_spread = sem("lo_spread")
        pos_done = sem("pos_done")
        pos_ready = sem("pos_ready")
        ring_zero = sem("ring_zero")
        broken_done = sem("broken_done")
        broken_summed = sem("broken_summed")
        path_known = sem("path_known")
        g_idx = sem("g_idx")
        g_gathered = sem("g_gathered")
        g_turned = sem("g_turned")
        g_copied = sem("g_copied")
        g_products = sem("g_products")
        g_step = sem("g_step")
        g_parts = sem("g_parts")
        idx_loaded = [sem(f"idx_loaded{h}") for h in range(2)]
        gathered = [sem(f"gathered{k}") for k in range(TPB)]
        types_ready = sem("types_ready")
        hot_ready = sem("hot_ready")
        tile_done = sem("tile_done")
        copied = sem("copied")
        added = sem("added")
        merged = sem("merged")
        cleared = sem("cleared")
        sums_done = sem("sums_done")
        agg_ready = sem("agg_ready")
        fin_done = sem("fin_done")
        ln = sem("ln")
        rooted = sem("rooted")
        x_blk_loaded = sem("x_blk_loaded")
        stored = sem("stored")

        def at_least(eng, s, v):
            if not isinstance(v, int) or v > 0:
                eng.wait_ge(s, v)

        def known(i, low):
            return not isinstance(i, int) or i >= low

        def seg_start(eng, block):
            if isinstance(block, int):
                return block % SEGS * SEG
            return eng.snap((block % SEGS) * SEG, min_val=0, max_val=(SEGS - 1) * SEG)

        def clear_ring(copy, segs):
            for s in segs:
                copy(ring[:, :, s * SEG:s * SEG + WIN], zeros[:])
                ins = copy(ring[:, :, s * SEG + BLOCK:(s + 1) * SEG], zeros[:])
            ins.then_inc(ring_zero, 1)

        def window(eng, regs, i, k):
            if k % POS_LOAD == 0:
                n = min(POS_LOAD, TPB - k)
                at = i * POS + k
                eng.load(regs[k:k + n], pos[0:1, at:at + n] if isinstance(i, int) else pos[0:1, bass.ds(at, n)])
            return eng.snap(regs[k], min_val=0, max_val=SEGS * SEG - WIN)

        def path(eng, in_order, in_general):
            eng.wait_ge(path_known, 1)
            which = eng.alloc_register(f"path_{eng.engine.name}")
            eng.load(which, general[0:1, 0:1])
            with eng.If_eq(which, 0):
                in_order()
            with eng.Else():
                in_general()

        def g_tiles(tile):
            def loop_on(eng):
                tile(0)
                with eng.Fori(1, TILES) as t:
                    tile(t)
            return loop_on

        def column(t):
            return slice(t, t + 1) if isinstance(t, int) else bass.ds(t, 1)

        def nodes(c):
            return slice(c * BLOCK, (c + 1) * BLOCK) if isinstance(c, int) else bass.ds(c * BLOCK, BLOCK)

        def g_finish(eng, step):
            step(3, False, False, False, True)
            with eng.Fori(4, BLOCKS + 1) as i:
                step(i, False, False, False, True)
            for i in range(BLOCKS + 1, BLOCKS + 3):
                step(i, False, False, False, True)

        block = ctx.enter_context(nc.Block())

        @block.sync
        def _(sp):
            for h, ks in enumerate(HALVES):
                sp.dma_start(idx[h][:], src_main[:, ks[0]:ks[-1] + 1]).then_inc(idx_loaded[h], 16)
            for t, main in ((dst, dst_main), (typ, type_main)):
                sp.dma_start(t[:, 0:FULL], main).then_inc(edges_loaded, 16)
            sp.wait_ge(padded, 1)
            for t, rest in ((dst, dst_rest), (typ, type_rest)):
                sp.dma_start(t[0:REST, FULL:FULL + 1], rest).then_inc(edges_loaded, 16)
            x_v = x.rearrange("(p n) d -> p n d", n=ROWS)
            for c in range(CHUNKS):
                n = slice(c * CHUNK, (c + 1) * CHUNK)
                sp.dma_start(x_all.rearrange("p (n d) -> p n d", d=D)[:, n], x_v[:, n]).then_inc(x_loaded[c], 16)
            sp.dma_start(loop[:], loop_w).then_inc(loop_loaded, 16)
            parts_v = x_parts.rearrange("(p n) c -> p n c", n=ROWS)
            for c in range(CHUNKS):
                n = slice(c * CHUNK, (c + 1) * CHUNK)
                sp.wait_ge(split_dve, c + 1)
                sp.dma_start(parts_v[:, n], parts_all[:, n].rearrange("p n c d -> p n (c d)").bitcast(F32)).then_inc(
                    parts_stored, 16)
            sp.wait_ge(pos_done, 1)
            sp.dma_start(pos[:].rearrange("o (b k) -> o b k", k=POS)[:, :, 0:TPB], pos_2d[:, 0:TPB]).then_inc(
                pos_ready, 16)

            def load_indices(i):
                for h, ks in enumerate(HALVES):
                    for k in ks:
                        sp.wait_ge(gathered[k], i * 16)
                    t = i * TPB + ks[0]
                    sp.dma_start(idx[h][:], src_main[:, t:t + len(ks)] if isinstance(i, int) else src[
                        :, bass.ds(t, len(ks))]).then_inc(idx_loaded[h], 16)

            load_indices(1)
            sp.dma_start(src[:, 0:FULL], src_main).then_inc(src_loaded, 16)
            sp.dma_start(src[0:REST, FULL:FULL + 1], src_rest).then_inc(src_loaded, 16)
            sp.wait_ge(first_split, len(HALVES))
            w_v = relation_w.rearrange("r d f -> d r f")
            for r in range(0, R, W_LOAD):
                sp.dma_start(w[:, r:r + W_LOAD, :], w_v[:, r:r + W_LOAD]).then_inc(w_loaded, 16)
            sp.wait_ge(const_done, 1)
            sp.dma_start(w[0:R, R, :], r_features).then_inc(w_loaded, 16)
            sp.dma_start(x_blk[:], x[0:P, :]).then_inc(x_blk_loaded, 16)

            sp.wait_ge(src_loaded, 2 * 16)

            def in_order():
                with sp.Fori(2, BLOCKS) as i:
                    load_indices(i)

            def g_load(t):
                if isinstance(t, int):
                    sp.wait_ge(idx_loaded[0], 2 * 16)
                else:
                    sp.wait_ge(g_step, t * G_STEPS + G_SETUP)
                sp.dma_start(idx[0][:, 0:1], src[:, column(t)]).then_inc(g_idx, 16)

            path(sp, in_order, lambda: g_tiles(g_load)(sp))

        @block.gpsimd
        def _(pool):
            nc.gpsimd.memset(src[:, FULL:], 0)
            nc.gpsimd.memset(typ[:, FULL:], 0)
            nc.gpsimd.memset(dst[:, FULL:], N).then_inc(padded, 1)
            nc.gpsimd.memset(head, N)
            nc.gpsimd.memset(head_next, N).then_inc(padded, 1)
            nc.gpsimd.memset(w[:, R, :], 0.0)
            nc.gpsimd.memset(ones[:], 1.0)
            nc.gpsimd.memset(ident[:], 0.0).then_inc(const_done, 1)
            nc.gpsimd.iota(iota_i, pattern=[[1, R * WIN]], base=0, channel_multiplier=0)
            nc.gpsimd.iota(blk_i, pattern=[[0, POS]], base=0, channel_multiplier=1).then_inc(iota_done, 1)
            pool.wait_ge(const_done, 1)
            nc.gpsimd.affine_select(out=ident[:], in_=ident[:], compare_op=ALU.not_equal, fill=1.0, base=0,
                                    pattern=[[-1, P]], channel_multiplier=1).then_inc(const_done, 1)

            for h, ks in enumerate(HALVES):
                pool.wait_ge(idx_loaded[h], 16)
                for k in ks:
                    pool.indirect_dma_start(
                        whole[:, k], None, x,
                        bass.IndirectOffsetOnAxis(ap=idx[h][:, k - ks[0]:k - ks[0] + 1], axis=0),
                    ).then_inc(gathered[k], 16)
            nc.gpsimd.memset(hot_type[:, :, R:], 0.0).then_inc(const_done, 1)
            pool.wait_ge(const_done, 2)
            pool.wait_ge(loop_loaded, 16)
            nc.gpsimd.tensor_tensor(loop[:], loop[:], ident[:], ALU.add).then_inc(loop_done, 1)

            free = [pool.alloc_register(f"free{h}") for h in range(2)]

            def gathers(i):
                for h, ks in enumerate(HALVES):
                    pool.wait_ge(idx_loaded[h], (i + 1) * 16)
                    if known(i, 2):
                        pool.wait_ge(tile_done, free[h])
                        pool.reg_add(free[1 - h], free[h], len(HALVES[1 - h]))
                    for k in ks:
                        pool.indirect_dma_start(
                            rows[:, k].rearrange("p c d -> p (c d)").bitcast(F32), None, x_parts,
                            bass.IndirectOffsetOnAxis(ap=idx[h][:, k - ks[0]:k - ks[0] + 1], axis=0),
                        ).then_inc(gathered[k], 16)

            def in_order():
                pool.wait_ge(parts_stored, CHUNKS * 16)
                gathers(1)
                pool.reg_mov(free[0], TPB + HALF)
                with pool.Fori(2, BLOCKS) as i:
                    gathers(i)

            def g_gather():
                pool.indirect_dma_start(g_rows, None, x, bass.IndirectOffsetOnAxis(ap=idx[0][:, 0:1], axis=0)).then_inc(
                    g_gathered, 16)

            def in_general():
                pool.wait_ge(g_step, G_SETUP)
                pool.wait_ge(g_idx, 16)
                g_gather()
                want, then = (pool.alloc_register(f"g_want{n}") for n in range(2))
                pool.reg_mov(then, 2 * 16)
                with pool.Fori(1, TILES):
                    pool.reg_mov(want, then)
                    pool.wait_ge(g_idx, want)
                    pool.reg_add(then, want, 16)
                    g_gather()

            path(pool, in_order, in_general)

        @block.scalar
        def _(act):
            act.wait_ge(padded, 2)
            for t, skip in ((head, 0), (head_next, 1)):
                whole_blocks, more = divmod(FULL - skip, TPB)
                act.dma_start(t[0:whole_blocks, 0:TPB], dst_main[0, skip:skip + whole_blocks * TPB].rearrange(
                    "(b k) -> b k", k=TPB)).then_inc(heads_loaded, 16)
                act.dma_start(t[whole_blocks:whole_blocks + 1, 0:more], dst_main[
                    0:1, skip + whole_blocks * TPB:FULL]).then_inc(heads_loaded, 16)
                act.dma_start(t[whole_blocks:whole_blocks + 1, more:more + 1], dst_rest[0:1, :]).then_inc(
                    heads_loaded, 16)
            for c in range(CHUNKS):
                n = slice(c * CHUNK, (c + 1) * CHUNK)
                m = slice(c * CHUNK * D, (c + 1) * CHUNK * D)
                act.wait_ge(x_loaded[c], 16)
                nc.scalar.copy(parts_all[:, n, 0, :], x_all[:, m].rearrange("p (n d) -> p n d", d=D)).then_inc(
                    split_act, 1)
            for ks in HALVES:
                for k in ks:
                    act.wait_ge(gathered[k], 16)
                at = slice(ks[0], ks[-1] + 1)
                nc.scalar.copy(first_rows[:, at, 0], whole[:, at]).then_inc(first_high, 1)
            regs = [act.alloc_register(f"act_pos{k}") for k in range(TPB)]

            def step(i, tiles, sums, late, fin):
                if tiles and isinstance(i, int):
                    act.wait_ge(pos_ready, 16)
                for k in range(TPB):
                    if tiles:
                        t = i * TPB + k
                        if k == 0:
                            if isinstance(i, int) and i == 0:
                                act.wait_ge(ring_zero, len(CLEARS))
                            if known(i, 1):
                                act.wait_ge(cleared, i)
                        start = window(act, regs, i, k)
                        act.wait_ge(tile_done, t + 1)
                        at_least(act, copied, t)
                        nc.scalar.copy(ring[:, :, bass.ds(start + 1, WIN - 1)],
                                       win_ps[bank_of(k)][:, :, 1:WIN]).then_inc(copied, 1)
                    if late and k == 8:
                        c = i - 2
                        if known(i, 3):
                            act.wait_ge(merged, i - 2)
                        at_least(act, fin_done, c)
                        if not tiles or not known(i, 3):
                            act.wait_ge(copied, min(i, BLOCKS) * TPB)
                            act.wait_ge(added, min(i, BLOCKS) * TPB)
                        s = seg_start(act, c)
                        nc.scalar.copy(cnt_sb[:], ring[:, R, bass.ds(s, BLOCK)] if not isinstance(s, int) else
                                       ring[:, R, s:s + BLOCK]).then_inc(agg_ready, 1)
                    if late and k == SUMS_LATE - 1:
                        act.wait_ge(sums_done, i - 1)
                        nc.scalar.copy(agg_sb[:], agg_ps[:]).then_inc(agg_ready, 1)
                    if fin:
                        c = i - 3
                        if k == 5:
                            act.wait_ge(ln, c * LN_STEPS + 1)
                            nc.scalar.sqrt(deg_root[:], deg[:]).then_inc(rooted, 1)
                        if k == 10 and known_less(i, BLOCKS + 2):
                            act.wait_ge(ln, c * LN_STEPS + 4)
                            nxt = x[(c + 1) * P:min((c + 2) * P, N), :] if isinstance(c, int) else x[
                                bass.ds((c + 1) * P, P), :]
                            act.dma_start(x_blk[0:nxt.shape[0], :], nxt).then_inc(x_blk_loaded, 16)
                        if k == 12:
                            act.wait_ge(ln, c * LN_STEPS + 8)
                            nc.scalar.sqrt(var_root[:], var_eps[:]).then_inc(rooted, 1)
                        if k == 16:
                            act.wait_ge(ln, (c + 1) * LN_STEPS)
                            to = out[c * P:min((c + 1) * P, N), :] if isinstance(c, int) else out[bass.ds(c * P, P), :]
                            act.dma_start(to, out_sb[0:to.shape[0], :]).then_inc(stored, 16)

            def known_less(i, high):
                return not isinstance(i, int) or i < high

            def g_turn(t):
                act.wait_ge(g_turned, t + 1)
                nc.scalar.copy(g_rows_t, g_turn_ps).then_inc(g_copied, 1)

            def g_finish_step(i, tiles, sums, late, fin):
                c = i - 3
                act.wait_ge(g_step, G_SETUP + TILES * G_STEPS)
                at_least(act, fin_done, c)
                nc.scalar.copy(cnt_sb[:], g_cnt[:, nodes(c)]).then_inc(agg_ready, 1)
                act.wait_ge(sums_done, c + 1)
                nc.scalar.copy(agg_sb[:], agg_ps[:]).then_inc(agg_ready, 1)
                step(i, tiles, sums, late, fin)

            def in_general():
                g_tiles(g_turn)(act)
                g_finish(act, g_finish_step)

            def in_order():
                act.wait_ge(parts_stored, CHUNKS * 16)
                act.wait_ge(pos_ready, 16)
                act.wait_ge(first_split, len(HALVES))
                clear_ring(nc.scalar.copy, CLEARS[1])
                run(act, step)

            path(act, in_order, in_general)
            act.wait_ge(stored, BLOCKS * 16)

        @block.vector
        def _(dve):
            done = [0]

            def chain(ins):
                done[0] += 1
                ins.then_inc(meta, 1)
                dve.wait_ge(meta, done[0])

            nc.vector.memset(zeros[:], 0.0)
            dve.wait_ge(iota_done, 1)
            nc.vector.tensor_copy(iota[:], iota_i)
            dve.wait_ge(edges_loaded, 4 * 16)
            nc.vector.tensor_copy(typ_f[:], typ)
            chain(nc.vector.tensor_copy(dst_f[:], dst))

            def split_x(chunks):
                for c in chunks:
                    n = slice(c * CHUNK, (c + 1) * CHUNK)
                    dve.wait_ge(split_act, c + 1)
                    nc.vector.tensor_tensor(
                        parts_all[:, n, 1, :], x_all.rearrange("p (n d) -> p n d", d=D)[:, n],
                        parts_all[:, n, 0, :].bitcast(F32), ALU.subtract).then_inc(split_dve, 1)

            split_x(range(EARLY))
            dve.wait_ge(lo_spread, 1)
            half = COLS_T // 2
            for b in range(2):
                c = slice(b * half, (b + 1) * half)
                ins = nc.vector.tensor_tensor(rel_f[:, c], dst_f[:, c], lo_ps[b][:, 0:half], ALU.subtract)
            chain(ins)
            chain(nc.vector.scalar_tensor_tensor(out=key_f[:], in0=typ_f[:], scalar=float(WIN), in1=rel_f[:],
                                                 op0=ALU.mult, op1=ALU.add))
            split_x(range(EARLY, CHUNKS))

            def split_first(h):
                at = slice(HALVES[h][0], HALVES[h][-1] + 1)
                dve.wait_ge(first_high, h + 1)
                nc.vector.tensor_tensor(first_rows[:, at, 1], whole[:, at], first_rows[:, at, 0].bitcast(F32),
                                        ALU.subtract).then_inc(
                    first_split, 1)

            split_first(0)
            first = half - 1
            nc.vector.tensor_tensor(after[:, 0:first], dst_f[:, 0:first], lo_ps[0][:, 1:half], ALU.subtract)
            chain(nc.vector.tensor_tensor(after[:, first:TILES], dst_f[:, first:TILES],
                                          lo_ps[1][:, 0:TILES - first], ALU.subtract))
            chain(nc.vector.memset(worst[:], 0.0))
            nc.vector.tensor_reduce(worst[:, 0:1], rel_f[:, 0:TILES], AX.X, ALU.min)
            nc.vector.tensor_reduce(worst[:, 1:2], after, AX.X, ALU.max)
            dve.wait_ge(heads_loaded, 6 * 16)
            tiles = slice(0, TPB)
            nc.vector.tensor_scalar(head_seg[:, tiles], head[:, tiles], 7, None, ALU.arith_shift_right)
            nc.vector.tensor_scalar(head_off[:, tiles], head[:, tiles], BLOCK - 1, None, ALU.bitwise_and)
            chain(nc.vector.tensor_tensor(head_gap[:, tiles], head_next[:, tiles], head[:, tiles], ALU.subtract))
            nc.vector.tensor_reduce(worst[0:BLOCKS, 2:3], head_gap[:, tiles], AX.X, ALU.max)
            nc.vector.tensor_copy(worst[0:1, 3:4], head[0:1, 0:1])
            chain(nc.vector.tensor_tensor(rounds[:, tiles], head_seg[:, tiles], blk_i[:, tiles], ALU.subtract))
            nc.vector.tensor_reduce(worst[0:BLOCKS, 4:5], rounds[:, tiles], AX.X, ALU.max)
            nc.vector.tensor_reduce(worst[0:BLOCKS, 5:6], rounds[:, tiles], AX.X, ALU.min)
            chain(nc.vector.tensor_reduce(worst[0:BLOCKS, 6:7], rounds[:, SAFE:TPB], AX.X, ALU.min))
            for n, (op, limit) in enumerate(((ALU.is_lt, 0), (ALU.is_gt, 0), (ALU.is_gt, WIN - 1), (ALU.is_gt, WIN - 1),
                                             (ALU.is_gt, 1), (ALU.is_lt, -1), (ALU.is_lt, 0))):
                ins = nc.vector.tensor_scalar(broken[:, n:n + 1], worst[:, n:n + 1], float(limit), None, op)
            ins.then_inc(broken_done, 1)
            dve.wait_ge(broken_summed, 1)
            chain(nc.vector.reduce_sum(broken_sum[:], broken_ps, AX.X))
            nc.vector.tensor_copy(general[0:1, 0:1], broken_sum[:]).then_inc(path_known, 1)
            nc.vector.scalar_tensor_tensor(out=head_off[:, tiles], in0=head_seg[:, tiles], scalar=float(SEG),
                                           in1=head_off[:, tiles], op0=ALU.mult, op1=ALU.add)
            chain(nc.vector.tensor_scalar(rounds[:, tiles], head_seg[:, tiles], float(ROUND_MULT), None, ALU.mult))
            chain(nc.vector.tensor_scalar(rounds[:, tiles], rounds[:, tiles], ROUND_SHIFT, None, ALU.arith_shift_right))
            nc.vector.scalar_tensor_tensor(out=pos_2d[:, tiles], in0=rounds[:, tiles], scalar=-float(SEGS * SEG),
                                           in1=head_off[:, tiles], op0=ALU.mult, op1=ALU.add).then_inc(pos_done, 1)
            regs = [dve.alloc_register(f"dve_pos{k}") for k in range(TPB)]

            def one_hot(t, buffer):
                nc.vector.tensor_scalar(hot[:, buffer], iota[:], key_f[:, column(t)], None, ALU.is_equal).then_inc(
                    hot_ready, 1)

            def one_hot_types(i, h):
                ks, t = HALVES[h], i * TPB + HALVES[h][0]
                n = len(ks)
                ts = slice(t, t + n) if isinstance(t, int) else bass.ds(t, n)
                at = slice(ks[0], ks[0] + n)
                nc.vector.tensor_tensor(
                    hot_node[:, at], iota[:, 0:WIN].unsqueeze(1).to_broadcast([P, n, WIN]),
                    rel_f[:, ts].unsqueeze(2).to_broadcast([P, n, WIN]), ALU.is_equal)
                nc.vector.tensor_tensor(
                    hot_type[:, at, 0:R], iota[:, 0:R].unsqueeze(1).to_broadcast([P, n, R]),
                    typ_f[:, ts].unsqueeze(2).to_broadcast([P, n, R]), ALU.is_equal).then_inc(types_ready, 1)

            def finish(c, k):
                if k == 3:
                    dve.wait_ge(fin_done, c + 1)
                    nc.vector.tensor_scalar(deg[:], fin_ps[:, D:D + 1], 1.0, None, ALU.max).then_inc(ln, 1)
                if k == 6:
                    dve.wait_ge(rooted, 2 * c + 1)
                    nc.vector.reciprocal(norm[:], deg_root[:]).then_inc(ln, 1)
                if k == 7:
                    dve.wait_ge(ln, c * LN_STEPS + 2)
                    nc.vector.tensor_scalar(h_sb[:], fin_ps[:, 0:D], norm[:], 0.0, ALU.mult, ALU.max).then_inc(ln, 1)
                if k == 8:
                    dve.wait_ge(ln, c * LN_STEPS + 3)
                    dve.wait_ge(x_blk_loaded, (c + 1) * 16)
                    nc.vector.tensor_tensor(y_sb[:], h_sb[:], x_blk[:], ALU.add).then_inc(ln, 1)
                if k == 9:
                    dve.wait_ge(ln, c * LN_STEPS + 4)
                    nc.vector.reduce_sum(y_sum[:], y_sb[:], AX.X).then_inc(ln, 1)
                    dve.wait_ge(ln, c * LN_STEPS + 5)
                    nc.vector.tensor_scalar(mean[:], y_sum[:], 1.0 / D, None, ALU.mult).then_inc(ln, 1)
                if k == 10:
                    dve.wait_ge(ln, c * LN_STEPS + 6)
                    nc.vector.tensor_scalar(y_mid[:], y_sb[:], mean[:], None, ALU.subtract).then_inc(ln, 1)
                if k == 11:
                    dve.wait_ge(ln, c * LN_STEPS + 7)
                    nc.vector.tensor_tensor_reduce(out=y_sq[:], in0=y_mid[:], in1=y_mid[:], scale=1.0 / D, scalar=EPS,
                                                   op0=ALU.mult, op1=ALU.add, accum_out=var_eps[:]).then_inc(ln, 1)
                if k == 13:
                    dve.wait_ge(rooted, 2 * c + 2)
                    nc.vector.reciprocal(rstd[:], var_root[:]).then_inc(ln, 1)
                if k == 14:
                    dve.wait_ge(ln, c * LN_STEPS + 9)
                    at_least(dve, stored, c * 16)
                    nc.vector.tensor_scalar(out_sb[:], y_mid[:], rstd[:], None, ALU.mult).then_inc(ln, 1)

            def merge(i, tiles):
                dve.wait_ge(added, i * TPB + SAFE if tiles else BLOCKS * TPB)
                if not tiles:
                    dve.wait_ge(copied, BLOCKS * TPB)
                head, tail = seg_start(dve, i - 1), seg_start(dve, i - 2)
                nc.vector.tensor_tensor(
                    ring[:, :, bass.ds(head, WIN)], ring[:, :, bass.ds(head, WIN)],
                    ring[:, :, bass.ds(tail + BLOCK, WIN)], ALU.add).then_inc(merged, 1)

            def clear(i):
                if known(i, 2):
                    dve.wait_ge(merged, i - 1)
                    dve.wait_ge(sums_done, i - 1)
                    dve.wait_ge(agg_ready, 2 * (i - 2) + 1)
                old = seg_start(dve, i - 2)
                nc.vector.tensor_copy(ring[:, :, bass.ds(old, WIN)], zeros[:])
                nc.vector.tensor_copy(ring[:, :, bass.ds(old + BLOCK, WIN)], zeros[:]).then_inc(cleared, 1)

            def step(i, tiles, sums, late, fin):
                c = i - 3
                for k in range(TPB):
                    if sums and known(i, 2) and k == SAFE:
                        merge(i, tiles)
                    if tiles:
                        t = i * TPB + k
                        if k == 4:
                            one_hot_types(i, 1)
                        if k == 14:
                            clear(i)
                        if k == 13:
                            one_hot_types(i + 1, 0)
                        one_hot(t + AHEAD, hot_of((k + AHEAD) % TPB))
                        start = window(dve, regs, i, k)
                        dve.wait_ge(copied, t + 1)
                        at_least(dve, added, t)
                        if k == 0 and known(i, 1):
                            dve.wait_ge(cleared, i)
                        a = ring[:, :, bass.ds(start, 1)]
                        nc.vector.tensor_tensor(a, a, win_ps[bank_of(k)][:, :, 0:1], ALU.add).then_inc(added, 1)
                    if fin:
                        finish(c, k)

            def in_order():
                one_hot_types(0, 0)
                for t in range(AHEAD):
                    one_hot(t, hot_of(t))
                split_first(1)
                dve.wait_ge(parts_stored, CHUNKS * 16)
                dve.wait_ge(pos_ready, 16)
                dve.wait_ge(first_split, len(HALVES))
                clear_ring(nc.vector.tensor_copy, CLEARS[0])
                dve.wait_ge(ring_zero, len(CLEARS))
                run(dve, step)

            def g_tile(t):
                n = [t * G_STEPS + G_SETUP]

                def then(ins):
                    n[0] = n[0] + 1
                    ins.then_inc(g_step, 1)
                    dve.wait_ge(g_step, n[0])

                then(nc.vector.tensor_scalar(g_mask, iota[:, 0:R], typ_f[:, column(t)], None, ALU.is_equal))
                then(nc.vector.tensor_scalar(g_type, iota[:, 0:P], typ_f[:, column(t)], None, ALU.is_equal))
                then(nc.vector.tensor_scalar(g_from, iota[:, 0:G_CHUNKS], -float(G_NODES), dst_f[:, column(t)], ALU.mult,
                                             ALU.add))
                for r in range(R):
                    if r % G_RELS == 0:
                        dve.wait_ge(g_products, t * G_GROUPS + r // G_RELS + 1)
                    product = g_prod_ps[:, r % G_RELS * D:(r % G_RELS + 1) * D]
                    if r == 0:
                        then(nc.vector.tensor_scalar(g_msg, product, g_mask[:, 0:1], None, ALU.mult))
                    else:
                        then(nc.vector.scalar_tensor_tensor(out=g_msg, in0=product, scalar=g_mask[:, r:r + 1], in1=g_msg,
                                                            op0=ALU.mult, op1=ALU.add))
                for q in range(G_CHUNKS):
                    then(nc.vector.tensor_scalar(g_hot, iota[:, 0:G_NODES], g_from[:, q:q + 1], None, ALU.is_equal))
                    dve.wait_ge(g_parts, t * G_CHUNKS + q + 1)
                    at = slice(q * G_NODES, (q + 1) * G_NODES)
                    then(nc.vector.tensor_tensor(g_agg[:, at], g_agg[:, at], g_agg_ps, ALU.add))
                    then(nc.vector.tensor_tensor(g_cnt[:, at], g_cnt[:, at], g_cnt_ps, ALU.add))

            def in_general():
                split_first(1)
                dve.wait_ge(parts_stored, CHUNKS * 16)
                dve.wait_ge(pos_ready, 16)
                dve.wait_ge(first_split, len(HALVES))
                nc.vector.memset(g_agg, 0.0).then_inc(g_step, 1)
                nc.vector.memset(g_cnt, 0.0).then_inc(g_step, 1)
                dve.wait_ge(g_step, G_SETUP)
                g_tiles(g_tile)(dve)
                g_finish(dve, step)

            path(dve, in_order, in_general)

        @block.tensor
        def _(pe):
            pe.wait_ge(meta, 1)
            pe.wait_ge(const_done, 2)
            half = COLS_T // 2
            for b in range(2):
                ins = nc.tensor.matmul(lo_ps[b][:, 0:half], ones[0:1, :], dst_f[0:1, b * half:(b + 1) * half],
                                       start=True, stop=True)
            ins.then_inc(lo_spread, 1)
            pe.wait_ge(broken_done, 1)
            nc.tensor.matmul(broken_ps, ones[:, 0:1], broken[:], start=True, stop=True).then_inc(broken_summed, 1)
            pe.wait_ge(const_done, 3)

            def tile(i, k):
                t = i * TPB + k
                if k % PAIR == 0:
                    if k in (0, HALF):
                        pe.wait_ge(types_ready, 2 * i + 1 + k // HALF)
                    pair = range(k, min(k + PAIR, TPB))
                    last = i * TPB + pair[-1]
                    if known(last, REUSE):
                        pe.wait_ge(added, last - REUSE + 1)
                    else:
                        pe.wait_ge(hot_ready, last + 1)
                    for n in pair:
                        nc.tensor.matmul(banks[bank_of(n)][:, R * WIN:COLS * WIN], hot_type[:, n], hot_node[:, n],
                                         start=True, stop=True)
                if known(i, 1):
                    pe.wait_ge(gathered[k], (i + 1) * 16)
                else:
                    pe.wait_ge(first_split, 1 if k < HALF else 2)
                from_rows = rows if known(i, 1) else first_rows
                for part in range(PARTS):
                    ins = nc.tensor.matmul(banks[bank_of(k)][:, 0:R * WIN], from_rows[:, k, part, :], hot[:, hot_of(k)],
                                           start=False, stop=(part == PARTS - 1), skip_group_check=True)
                ins.then_inc(tile_done, 1)

            def relations(slot, seg):
                rs = range(COLS * slot // slots, COLS * (slot + 1) // slots)
                for r in rs:
                    ins = nc.tensor.matmul(agg_ps[:], w[:, r, :], ring[:, r, bass.ds(seg, BLOCK)], start=(r == 0),
                                           stop=(r == COLS - 1))
                if COLS - 1 in rs:
                    ins.then_inc(sums_done, 1)

            slots = TPB - SUMS_FROM + SUMS_LATE

            def step(i, tiles, sums, late, fin):
                if late:
                    last_seg = seg_start(pe, i - 2)
                if sums:
                    seg = seg_start(pe, i - 1)
                for k in range(TPB):
                    if tiles:
                        tile(i, k)
                    if fin and k == 2:
                        c = i - 3
                        pe.wait_ge(agg_ready, 2 * (c + 1))
                        at_least(pe, ln, (c - 1) * LN_STEPS + 3)
                        if isinstance(c, int) and c == 0:
                            pe.wait_ge(loop_done, 1)
                        nc.tensor.matmul(fin_ps[:, D:D + 1], cnt_sb[:], ones[:, 0:1], start=True, stop=True)
                        nc.tensor.matmul(fin_ps[:, 0:D], agg_sb[:], loop[:], start=True, stop=True).then_inc(fin_done, 1)
                    if late and k < SUMS_LATE:
                        relations(TPB - SUMS_FROM + k, last_seg)
                    if sums and k >= SUMS_FROM:
                        if k == SUMS_FROM:
                            if known(i, 2):
                                pe.wait_ge(merged, i - 1)
                            else:
                                pe.wait_ge(added, i * TPB + SAFE)
                                pe.wait_ge(w_loaded, W_LOADS * 16)
                            at_least(pe, agg_ready, 2 * (i - 1))
                        relations(k - SUMS_FROM, seg)

            def g_tile(t):
                pe.wait_ge(g_gathered, (t + 1) * 16)
                nc.tensor.transpose(g_turn_ps, g_rows, ident[:]).then_inc(g_turned, 1)
                pe.wait_ge(g_copied, t + 1)
                for j in range(G_GROUPS):
                    at_least(pe, g_step, t * G_STEPS + G_SETUP + 3 + j * G_RELS)
                    nc.tensor.matmul(g_prod_ps[:], g_rows_t,
                                     w[:, j * G_RELS:(j + 1) * G_RELS, :].rearrange("p r f -> p (r f)"),
                                     start=True, stop=True).then_inc(g_products, 1)
                for q in range(G_CHUNKS):
                    pe.wait_ge(g_step, t * G_STEPS + G_SETUP + 3 + R + 3 * q + 1)
                    nc.tensor.matmul(g_agg_ps, g_msg, g_hot, start=True, stop=True)
                    nc.tensor.matmul(g_cnt_ps, g_type, g_hot, start=True, stop=True).then_inc(g_parts, 1)

            def g_finish_step(i, tiles, sums, late, fin):
                c = i - 3
                pe.wait_ge(g_step, G_SETUP + TILES * G_STEPS)
                at_least(pe, agg_ready, 2 * c)
                nc.tensor.matmul(agg_ps[:], w[:, R, :], g_cnt[:, nodes(c)], start=True, stop=False)
                nc.tensor.matmul(agg_ps[:], ident[:], g_agg[:, nodes(c)], start=False, stop=True).then_inc(sums_done, 1)
                step(i, tiles, sums, late, fin)

            def in_general():
                pe.wait_ge(w_loaded, W_LOADS * 16)
                g_tiles(g_tile)(pe)
                g_finish(pe, g_finish_step)

            path(pe, lambda: run(pe, step), in_general)


def run(eng, step):
    for i in range(4):
        step(i, True, i >= 1, i >= 2, i >= 3)
    with eng.Fori(4, BLOCKS) as i:
        step(i, True, True, True, True)
    for i in range(BLOCKS, BLOCKS + 3):
        step(i, False, i < BLOCKS + 1, i < BLOCKS + 2, True)


_OUT = (N, D)


def kernel(x, src, dst, edge_type_40, L0_gnn_rFeatures, L0_gnn_relation_weights, L0_gnn_loop_weight):
    import numpy as np
    import concourse.bacc as bacc
    from concourse.bass_utils import run_bass_kernel_spmd

    nc = bacc.Bacc("TRN2", target_bir_lowering=False, num_devices=1)
    arrays = {"x": np.ascontiguousarray(x)}
    for name, a in (("src", src), ("dst", dst), ("type", edge_type_40)):
        a = np.asarray(a)
        arrays[f"{name}_main"] = np.ascontiguousarray(a[:FULL * P].reshape(FULL, P).T)
        arrays[f"{name}_rest"] = np.ascontiguousarray(a[FULL * P:].reshape(REST, 1))
    arrays["r_features"] = np.ascontiguousarray(L0_gnn_rFeatures)
    arrays["relation_w"] = np.ascontiguousarray(L0_gnn_relation_weights)
    arrays["loop_w"] = np.ascontiguousarray(L0_gnn_loop_weight)
    args = [nc.dram_tensor(k, a.shape, mybir.dt.from_np(a.dtype), kind="ExternalInput").ap() for k, a in arrays.items()]
    out = nc.dram_tensor("out", _OUT, F32, kind="ExternalOutput").ap()
    build(nc, *args, out)
    r = run_bass_kernel_spmd(nc, [arrays], core_ids=[0])
    return r.results[0]["out"]
```
